# Optimizing a Trainium2 kernel written in Bass

```python
import numpy as np
import jax
import jax.numpy as jnp

def _softmax(x, axis=-1):
    return jax.nn.softmax(x, axis=axis)

def _gelu(x):
    return jax.nn.gelu(x, approximate=True)

def _silu(x):
    return jax.nn.silu(x)

def _sigmoid(x):
    return jax.nn.sigmoid(x)

def _layernorm(x, axis=-1, eps=1e-05):
    m = jnp.mean(x, axis=axis, keepdims=True)
    v = jnp.var(x, axis=axis, keepdims=True)
    return (x - m) / jnp.sqrt(v + eps)

def _scatter_add(tgt, idx, src, axis=0):
    return tgt.at[idx].add(src)

def _segment_sum(src, seg, n):
    return jax.ops.segment_sum(src, seg, n)
kernel_name = 'mk_hybrid_d1_jaxref_r8_035f88'

def setup_inputs(seed: int=0):
    np.random.seed(seed)
    _w = jnp.asarray

    def _L0_attn_a_setup():
        import jax, jax.numpy as jnp
        import numpy as np
        B, T, C = (4, 512, 128)
        H = 16
        D = C // H
        EPS = 1e-06

        def _phi(x):
            return jax.nn.elu(x) + 1.0
        key = jax.random.key(seed)
        k1, k2, k3 = jax.random.split(key, 3)
        x = jax.random.normal(k1, (B, T, C), dtype=jnp.float32)
        Wqkv = jax.random.normal(k2, (3 * C, C), dtype=jnp.float32) * (1.0 / np.sqrt(C))
        Wproj = jax.random.normal(k3, (C, C), dtype=jnp.float32) * (1.0 / np.sqrt(C))
        bproj = jnp.zeros((C,), dtype=jnp.float32)
        return {'x': x, 'Wqkv': Wqkv, 'Wproj': Wproj, 'bproj': bproj}
    _L0_attn_a_in = _L0_attn_a_setup()

    def _L0_attn_b_setup():
        import jax, jax.numpy as jnp
        import numpy as np

        def _rope_tables(T, d):
            half = d // 2
            i = jnp.arange(half, dtype=jnp.float32)
            theta = 10000.0 ** (-2.0 * i / d)
            m = jnp.arange(T, dtype=jnp.float32)[:, None]
            ang = m * theta[None, :]
            return (jnp.cos(ang), jnp.sin(ang))

        def _rotate(v, cos, sin):
            B, T, d = v.shape
            half = d // 2
            v2 = v.reshape(B, T, half, 2)
            even, odd = (v2[..., 0], v2[..., 1])
            c = cos[None, :, :]
            s = sin[None, :, :]
            new_even = even * c - odd * s
            new_odd = even * s + odd * c
            return jnp.stack([new_even, new_odd], axis=-1).reshape(B, T, d)
        key = jax.random.key(seed)
        k1, k2, k3, k4 = jax.random.split(key, 4)
        B, T, d = (4, 256, 128)
        x = jax.random.normal(k1, (B, T, d), dtype=jnp.float32)
        scale = 0.02
        Wq = jax.random.normal(k2, (d, d), dtype=jnp.float32) * scale
        Wk = jax.random.normal(k3, (d, d), dtype=jnp.float32) * scale
        Wv = jax.random.normal(k4, (d, d), dtype=jnp.float32) * scale
        return {'x': x, 'Wq': Wq, 'Wk': Wk, 'Wv': Wv}
    _L0_attn_b_in = _L0_attn_b_setup()

    def _L0_ffn_setup():
        import jax, jax.numpy as jnp
        import numpy as np
        import math
        BETA = 0.9
        THRESHOLD = 1.0
        NUM_STEPS = 5
        ALPHA = 2.0

        @jax.custom_vjp
        def spike_fn(u):
            return (u > 0).astype(u.dtype)

        def _spike_fwd(u):
            return (spike_fn(u), u)

        def _spike_bwd(u, g):
            s = jnp.pi / 2.0 * ALPHA * u
            return (g * (ALPHA / 2.0) / (1.0 + s * s),)
        spike_fn.defvjp(_spike_fwd, _spike_bwd)
        key = jax.random.key(seed)
        k1, k2, k3 = jax.random.split(key, 3)
        n_embd = 128
        x = jax.random.normal(k1, (4, 256, n_embd), dtype=jnp.float32)
        W_fc = jax.random.normal(k2, (4 * n_embd, n_embd), dtype=jnp.float32) / math.sqrt(n_embd)
        W_proj = jax.random.normal(k3, (n_embd, 4 * n_embd), dtype=jnp.float32) / math.sqrt(4 * n_embd)
        return {'x': x, 'W_fc': W_fc, 'W_proj': W_proj}
    _L0_ffn_in = _L0_ffn_setup()
    _d = {'L0_attn_a_x': _L0_attn_a_in['x'], 'L0_attn_a_Wqkv': _L0_attn_a_in['Wqkv'], 'L0_attn_a_Wproj': _L0_attn_a_in['Wproj'], 'L0_attn_a_bproj': _L0_attn_a_in['bproj'], 'L0_attn_b_Wq': _L0_attn_b_in['Wq'], 'L0_attn_b_Wk': _L0_attn_b_in['Wk'], 'L0_attn_b_Wv': _L0_attn_b_in['Wv'], 'L0_ffn_W_fc': _L0_ffn_in['W_fc'], 'L0_ffn_W_proj': _L0_ffn_in['W_proj']}
    _x0 = _d['L0_attn_a_x']
    _d['L0_attn_a_x'] = jax.random.normal(jax.random.fold_in(jax.random.key(seed), 1), (1, 2048, 128), dtype=_x0.dtype)
    del _x0
    return _d

def reference(L0_attn_a_x, L0_attn_a_Wqkv, L0_attn_a_Wproj, L0_attn_a_bproj, L0_attn_b_Wq, L0_attn_b_Wk, L0_attn_b_Wv, L0_ffn_W_fc, L0_ffn_W_proj):

    def _L0_attn_a_ref(x, Wqkv, Wproj, bproj):
        import jax, jax.numpy as jnp
        import numpy as np
        B, T, C = (4, 512, 128)
        H = 16
        D = C // H
        EPS = 1e-06

        def _phi(x):
            return jax.nn.elu(x) + 1.0
        b, t, c = x.shape
        qkv = jnp.einsum('btc,ec->bte', x, Wqkv)
        qkv = qkv.reshape(b, t, 3, H, D)
        q, k, v = (qkv[:, :, 0], qkv[:, :, 1], qkv[:, :, 2])
        q = _phi(q)
        k = _phi(k)
        kv = jnp.einsum('bnhd,bnhm->bhdm', k, v)
        k_sum = k.sum(axis=1)
        out = jnp.einsum('bnhd,bhdm->bnhm', q, kv)
        normalizer = jnp.einsum('bnhd,bhd->bnh', q, k_sum) + EPS
        out = out / normalizer[..., None]
        out = out.reshape(b, t, c)
        out = jnp.einsum('btc,oc->bto', out, Wproj) + bproj
        return out

    def _L0_attn_b_ref(x, Wq, Wk, Wv):
        import jax, jax.numpy as jnp
        import numpy as np

        def _rope_tables(T, d):
            half = d // 2
            i = jnp.arange(half, dtype=jnp.float32)
            theta = 10000.0 ** (-2.0 * i / d)
            m = jnp.arange(T, dtype=jnp.float32)[:, None]
            ang = m * theta[None, :]
            return (jnp.cos(ang), jnp.sin(ang))

        def _rotate(v, cos, sin):
            B, T, d = v.shape
            half = d // 2
            v2 = v.reshape(B, T, half, 2)
            even, odd = (v2[..., 0], v2[..., 1])
            c = cos[None, :, :]
            s = sin[None, :, :]
            new_even = even * c - odd * s
            new_odd = even * s + odd * c
            return jnp.stack([new_even, new_odd], axis=-1).reshape(B, T, d)
        B, T, d = x.shape
        cos, sin = _rope_tables(T, d)
        Q = jnp.einsum('btd,ed->bte', x, Wq)
        K = jnp.einsum('btd,ed->bte', x, Wk)
        V = jnp.einsum('btd,ed->bte', x, Wv)
        Qr = _rotate(Q, cos, sin)
        Kr = _rotate(K, cos, sin)
        scores = jnp.einsum('bqd,bkd->bqk', Qr, Kr) / jnp.sqrt(jnp.float32(d))
        mask = jnp.tril(jnp.ones((T, T), dtype=bool), k=1)
        scores = jnp.where(mask[None, :, :], scores, -jnp.inf)
        attn = jax.nn.softmax(scores, axis=-1)
        out = jnp.einsum('bqk,bkd->bqd', attn, V)
        return out

    def _L0_ffn_ref(x, W_fc, W_proj):
        import jax, jax.numpy as jnp
        import numpy as np
        import math
        BETA = 0.9
        THRESHOLD = 1.0
        NUM_STEPS = 5
        ALPHA = 2.0

        @jax.custom_vjp
        def spike_fn(u):
            return (u > 0).astype(u.dtype)

        def _spike_fwd(u):
            return (spike_fn(u), u)

        def _spike_bwd(u, g):
            s = jnp.pi / 2.0 * ALPHA * u
            return (g * (ALPHA / 2.0) / (1.0 + s * s),)
        spike_fn.defvjp(_spike_fwd, _spike_bwd)
        h = jnp.square(jax.nn.relu(jnp.einsum('bsd,fd->bsf', x, W_fc)))
        y = jnp.einsum('bsf,df->bsd', h, W_proj)

        def step(mem, _):
            reset = jax.lax.stop_gradient(spike_fn(mem - THRESHOLD))
            mem_new = BETA * mem + y - reset * THRESHOLD
            spk = spike_fn(mem_new - THRESHOLD)
            return (mem_new, spk)
        mem0 = jnp.zeros_like(y)
        _, spks = jax.lax.scan(step, mem0, None, length=NUM_STEPS)
        return jnp.sum(spks, axis=0) / NUM_STEPS
    x = L0_attn_a_x
    x = x + _L0_attn_a_ref(_layernorm(x, axis=-1), L0_attn_a_Wqkv, L0_attn_a_Wproj, L0_attn_a_bproj)
    x = x + _L0_ffn_ref(_layernorm(x, axis=-1), L0_ffn_W_fc, L0_ffn_W_proj)
    x = x + _L0_attn_b_ref(_layernorm(x, axis=-1), L0_attn_b_Wq, L0_attn_b_Wk, L0_attn_b_Wv)
    x = x + _L0_ffn_ref(_layernorm(x, axis=-1), L0_ffn_W_fc, L0_ffn_W_proj)
    return x

_drawn_inputs = setup_inputs


def setup_inputs(seed=0):
    import zlib

    import numpy as np

    out = dict(_drawn_inputs(seed))
    spreads = {'L0_attn_a_bproj': (0.0, 0.1)}
    factors = {'L0_attn_b_Wq': 8.0, 'L0_attn_b_Wk': 8.0}
    for name, (base, spread) in spreads.items():
        noise = np.random.default_rng([zlib.crc32(name.encode()), seed]).standard_normal(out[name].shape)
        drawn = base * np.exp(spread * noise) if base else spread * noise
        out[name] = jnp.asarray(drawn.astype(out[name].dtype))
    for name, factor in factors.items():
        out[name] = (out[name] * factor).astype(out[name].dtype)
    return out
```

```python
from contextlib import ExitStack

import numpy as np

import concourse.bass as bass
from concourse import mybir

F32 = mybir.dt.float32
F32R = mybir.dt.float32r
BF16 = mybir.dt.bfloat16
ALU = mybir.AluOpType
ACT = mybir.ActivationFunctionType
AX_X = mybir.AxisListType.X

P = 128
C = 128
N_TOK = 2048
T = N_TOK // P
TG = 4
G = T // TG
W = TG * P
HEADS = 16
HD = C // HEADS
F = 512
M = F // P
HALF = C // 2
EPS_LN = 1e-5
EPS_ATT = 1e-6
SCALE = float(1.0 / np.sqrt(np.float32(C)))
BETA, THRESHOLD, STEPS = 0.9, 1.0, 5
MASKED = -3.0e38
EXTRA = 1
MASK_LEAD = W - P
MASK_W = MASK_LEAD + 2 * P
EXP_PIECE = 1024
JUST_BELOW_1 = 1.0 - 2.0 ** -24


def score_chunks(i):
    width = N_TOK if i == T - 1 else max(256, P * (i + 1) + 2 * EXTRA)
    cuts, at = [], 0
    while width - at > W:
        step = W if width - at - W >= 256 else width - at - 256
        cuts.append((at, at + step))
        at += step
    cuts.append((at, width))
    return cuts


def exp_pieces(i):
    width = score_chunks(i)[-1][1]
    return [(a, min(a + EXP_PIECE, width)) if width - a - EXP_PIECE > 256 else (a, width)
            for a in range(0, width, EXP_PIECE) if a == 0 or width - (a - EXP_PIECE) - EXP_PIECE > 256]


def make_plan():
    plan = []

    def head(lane, g):
        plan.append(("stats", lane, g))
        plan.append(("norm", lane, g))

    head(0, 0)
    plan.append(("turn", 0, 0))
    head(0, 1)
    for g in range(G):
        plan.append(("q", g))
        plan.append(("kv", g))
        plan.append(("bias", g))
        if g + 1 < G:
            plan.append(("turn", 0, g + 1))
        if g + 2 < G:
            head(0, g + 2)
        if g >= 1:
            plan.append(("acc", g - 1))
    plan.append(("acc", G - 1))
    plan.append(("diag",))
    for tick in range(G + 1):
        now, last = tick, tick - 1
        if last >= 0:
            plan.extend([("f2", last), ("spike", last)])
        if now < G:
            plan.extend([("ao", now), ("at", now), ("pr", now)])
            head(1, now)
            plan.extend([("turn", 1, now), ("f1", now)])
        if last >= 0:
            plan.append(("count", last))
            head(2, last)
            plan.extend([("turn", 2, last), ("qkv", last), ("rope", last), ("tqk", last)])
    plan.append(("s", 0))
    plan.append(("e", 0))
    for i in range(T):
        if i + 1 < T:
            plan.append(("s", i + 1))
        jgs = i // TG + 1
        plan.append(("t", i, 0))
        for jg in range(jgs):
            if jg + 1 < jgs:
                plan.append(("t", i, jg + 1))
            if jg == 0 and i + 1 < T:
                plan.append(("e", i + 1))
            plan.append(("pv", i, jg))
        plan.append(("o", i))
        done = i - 1
        if done >= TG and (done - TG) % TG < 3 and (done - TG) // TG < G - 1:
            g, part = (done - TG) // TG, (done - TG) % TG
            if part == 0:
                head(3, g)
                plan.append(("turn", 3, g))
            elif part == 1:
                plan.append(("f1", G + g))
            else:
                plan.extend([("f2", G + g), ("spike", G + g), ("count", G + g), ("store", g)])
    for g in range(G):
        if ("stats", 3, g) not in plan:
            head(3, g)
            plan.append(("turn", 3, g))
        if ("f1", G + g) not in plan:
            plan.append(("f1", G + g))
        if ("f2", G + g) not in plan:
            plan.extend([("f2", G + g), ("spike", G + g), ("count", G + g), ("store", g)])
    return plan


def hybrid_block(nc, x, w_qkv, w_proj, b_proj, w_fc, w_down, w_rope, cos, sin, ident, mask, heads, out):
    plan = make_plan()
    chunk_no, piece_no, turn_no = {}, {}, {}
    for step in plan:
        if step[0] == "s":
            for c in range(len(score_chunks(step[1]))):
                chunk_no[step[1], c] = len(chunk_no)
        if step[0] == "e":
            for p in range(len(exp_pieces(step[1]))):
                piece_no[step[1], p] = len(piece_no)
        if step[0] == "t":
            turn_no[step[1:]] = len(turn_no)

    with ExitStack() as ctx:
        def sb(name, *shape, dt=F32):
            return ctx.enter_context(nc.sbuf_tensor(name, [P, *shape], dt))

        def sem(name):
            return ctx.enter_context(nc.semaphore(name))

        def sems(name, n):
            return [sem(f"{name}{i}") for i in range(n)]

        S0, S1, P0, P1, O, H0, H1, MB = (
            ctx.enter_context(nc.psum_tensor(f"bank_{n}", [P, W], F32))
            for n in ("s0", "s1", "p0", "p1", "o", "h0", "h1", "m"))

        xs = sb("xs", T, C)
        stat = sb("stat", 4, T, 6)
        mom = sb("mom", 4, T, 2)
        veps = sb("veps", 4, T)
        rstd = sb("rstd", 4, T)
        nmean = sb("nmean", 4, T)
        nmr = sb("nmr", 4, T)
        mhalf = sb("mhalf", TG)
        xn = [sb(f"xn{k}", 2, TG, C) for k in range(2)]
        xh = [sb(f"xh{k}", 2, W, dt=F32R) for k in range(2)]
        xl = [sb(f"xl{k}", 2, W, dt=F32R) for k in range(2)]
        ebuf = sb("ebuf", 2, W)
        rbuf = sb("rbuf", 2, W)
        qphi = sb("qphi", N_TOK)
        kphi = sb("kphi", N_TOK)
        vone = sb("vone", T, C + 1)
        bdkv = sb("bdkv", C)
        bdks = sb("bdks", HEADS)
        den = sb("den", TG * HEADS)
        rec = sb("rec", TG * HEADS)
        relu = sb("relu", 2, W)
        ek, rk = (relu[:, k, :].rearrange("p (r t c) -> p r t c", r=2, t=2) for k in range(2))
        hid = sb("hid", 2, M, W)
        y = sb("y", 2, W)
        u = sb("u", W)
        mem = sb("mem", 2, W)
        sign = sb("sign", STEPS, W, dt=BF16)
        half_id = sb("half_id", P, dt=BF16)
        fives = sb("fives", P, dt=BF16)
        ones = sb("ones", W, dt=BF16)
        above = sb("above", 1)
        qk = sb("qk", 2, TG, 2 * C)
        rot = sb("rot", 2, TG, 2 * C)
        rsin = sb("rsin", TG, 2 * C)
        cos_sb = sb("cos_sb", 2, TG, C)
        sin_sb = sb("sin_sb", 2, TG, C)
        qh, ql, kh, kl = (sb(n, N_TOK, dt=F32R) for n in ("qh", "ql", "kh", "kl"))
        v = sb("v", T, C)
        vnext = sb("vnext", T, C)
        cmax = sb("cmax", T, 4)
        negm = sb("negm", T)
        psums = sb("psums", T, 2)
        psum_all = sb("psum_all", T)
        rsum = sb("rsum", T)
        pt = sb("pt", 3, W)
        osb = sb("osb", 2, C)
        WA, WF, WR = 3 * C, F, 3 * C
        wh = sb("wh", WA + WF + WR, dt=F32R)
        wl = sb("wl", WA + WF + WR, dt=F32R)
        wp = sb("wp", C)
        wd = sb("wd", M, C)
        bias = sb("bias", C)
        id_sb = sb("id_sb", P)
        mask_sb = sb("mask_sb", MASK_W)
        heads_sb = sb("heads_sb", C + HEADS)
        raw = hid[:].rearrange("p a m w -> p (a m w)")[:, 0:WA + WF + WR]
        a_of, f_of, r_of = 0, WA, WA + WF
        scores = [qphi, kphi]

        x_in = sems("x_in", G)
        wa_in, wf_in, wr_in, id_in, small_in, wd_in, mask_in = (
            sem(n) for n in ("wa_in", "wf_in", "wr_in", "id_in", "small_in", "wd_in", "mask_in"))
        trig_in = sems("trig_in", G)
        vnext_in, stored = sem("vnext_in"), sem("stored")
        w_hi, w_lo, consts = sem("w_hi"), sem("w_lo"), sem("consts")
        vnext_zero, vone_set = sem("vnext_zero"), sem("vone_set")
        bn_done, mom_ready, veps_ready, rstd_ready, nmr_ready, xn_ready = (
            sems(n, 4) for n in ("bn_done", "mom_ready", "veps_ready", "rstd_ready", "nmr_ready", "xn_ready"))
        xT_ready, hi_ready, lo_ready = (sems(n, 2) for n in ("xT_ready", "hi_ready", "lo_ready"))
        (q_ready, eq_ready, rq_ready, qphi_ready, kv_ready, ek_ready, rk_ready, vone_ready, kphi_ready, sum_ready,
         diag_ready, ao_ready, den_ready, rec_ready, heads_ready, aT_ready, aTs_ready, pr_ready, xb_ready,
         x1_ready) = (sem(n) for n in (
             "q_ready", "eq_ready", "rq_ready", "qphi_ready", "kv_ready", "ek_ready", "rk_ready", "vone_ready",
             "kphi_ready", "sum_ready", "diag_ready", "ao_ready", "den_ready", "rec_ready", "heads_ready",
             "aT_ready", "aTs_ready", "pr_ready", "xb_ready", "x1_ready"))
        h_ready, relu_ready, sq_ready, y_ready, ysb_ready, mem_ready, sign_ready, count_ready, xf_ready = (
            sem(n) for n in ("h_ready", "relu_ready", "sq_ready", "y_ready", "ysb_ready", "mem_ready",
                             "sign_ready", "count_ready", "xf_ready"))
        (qkv_ready, v_ready, cosd, sind, half_ready, tqk_ready, qkhi_ready, qklo_ready, s_ready, sc_ready,
         m_ready, e_ready, pt_ready, ptc_ready, pv_ready, ps_ready, rs_ready, osb_ready, x3_ready) = (
             sem(n) for n in (
                 "qkv_ready", "v_ready", "cosd", "sind", "half_ready", "tqk_ready", "qkhi_ready", "qklo_ready",
                 "s_ready", "sc_ready", "m_ready", "e_ready", "pt_ready", "ptc_ready", "pv_ready",
                 "ps_ready", "rs_ready", "osb_ready", "x3_ready"))

        NORM_ON_ACT = (False, True, True, True)

        def lane_job(norm, g):
            return norm % 2, G * (norm // 2) + g

        def lane_used(eng, lane, j):
            if j < 2:
                return
            if lane == 1:
                eng.wait_ge(h_ready, M * (j - 1))
            elif j - 2 < G:
                eng.wait_ge(kv_ready, 2 * (j - 1))
            else:
                eng.wait_ge(qkv_ready, TG * (j - 1 - G))

        block = ctx.enter_context(nc.Block())

        @block.sync
        def _(sp):
            x_t = x.rearrange("(t p) c -> p t c", p=P)
            o_t = out.rearrange("(t p) c -> p t c", p=P)
            for g in range(G):
                sp.dma_start(xs[:, TG * g:TG * g + TG, :], x_t[:, TG * g:TG * g + TG, :]).then_inc(x_in[g], 16)
            sp.dma_start(wd[:].rearrange("p m c -> p (m c)"), w_down).then_inc(wd_in, 16)
            for step in plan:
                if step[0] == "norm" and step[1] == 2:
                    g = step[2]
                    if g >= 2:
                        sp.wait_ge(cosd, g - 1)
                        sp.wait_ge(sind, g - 1)
                    for dst, src in ((cos_sb, cos), (sin_sb, sin)):
                        sp.dma_start(dst[:, g % 2], src.rearrange("(t p) c -> p t c", p=P)[
                            :, TG * g:TG * g + TG, :]).then_inc(trig_in[g], 16)
                if step[0] == "rope":
                    g = step[1]
                    sp.wait_ge(v_ready, TG * (g + 1))
                    sp.wait_ge(vnext_zero, 1)
                    a = max(1, TG * g)
                    sp.dma_start(vnext[P - 1:P, a - 1:TG * g + TG - 1, :],
                                 v[0:1, a:TG * g + TG, :]).then_inc(vnext_in, 16)
                if step[0] == "store":
                    g = step[1]
                    sp.wait_ge(xf_ready, G + g + 1)
                    sp.dma_start(o_t[:, TG * g:TG * g + TG, :], xs[:, TG * g:TG * g + TG, :]).then_inc(stored, 16)
            sp.wait_ge(stored, 16 * G)

        @block.gpsimd
        def _(pool):
            pool.dma_start(raw[:, f_of:f_of + WF], w_fc).then_inc(wf_in, 16)
            pool.dma_start(raw[:, r_of:r_of + WR], w_rope).then_inc(wr_in, 16)
            pool.dma_start(mask_sb[:], mask).then_inc(mask_in, 16)
            nc.gpsimd.memset(mhalf[:], -0.5)
            nc.gpsimd.memset(above[:], -1.0)
            nc.gpsimd.memset(fives[:], STEPS / 2 / P)
            nc.gpsimd.memset(ones[:], 1.0)
            pool.wait_ge(id_in, 16)
            nc.gpsimd.tensor_scalar(half_id[:], id_sb[:], 0.5, None, ALU.mult).then_inc(consts, 1)
            for step in plan:
                if step[0] == "stats":
                    n, g = step[1:]
                    ts = slice(TG * g, TG * g + TG)
                    pool.wait_ge(mom_ready[n], g + 1)
                    nc.gpsimd.tensor_scalar_add(veps[:, n, ts], mom[:, n, ts, 1], EPS_LN).then_inc(veps_ready[n], 1)
                    nc.gpsimd.tensor_scalar(nmean[:, n, ts], mom[:, n, ts, 0], -1.0, None, ALU.mult).then_inc(
                        veps_ready[n], 1)
                    pool.wait_ge(veps_ready[n], 2 * (g + 1))
                    pool.wait_ge(consts, 1)
                    nc.gpsimd.tensor_tensor(rstd[:, n, ts], veps[:, n, ts], mhalf[:], ALU.pow).then_inc(rstd_ready[n], 1)
                    if NORM_ON_ACT[n]:
                        pool.wait_ge(rstd_ready[n], g + 1)
                        nc.gpsimd.tensor_tensor(nmr[:, n, ts], nmean[:, n, ts], rstd[:, n, ts],
                                                ALU.mult).then_inc(nmr_ready[n], 1)
                elif step[0] == "bias":
                    g = step[1]
                    pool.wait_ge(xn_ready[0], g + 1)
                    if g == 0:
                        pool.wait_ge(small_in, 48)
                    xg = xs[:, TG * g:TG * g + TG, :]
                    nc.gpsimd.tensor_tensor(xg, xg, bias[:].unsqueeze(1).to_broadcast([P, TG, C]),
                                            ALU.add).then_inc(xb_ready, 1)
                    if g == 0:
                        nc.gpsimd.memset(vnext[:], 0.0).then_inc(vnext_zero, 1)
                elif step[0] == "rope":
                    g = step[1]
                    pool.wait_ge(v_ready, TG * (g + 1))
                    pool.wait_ge(trig_in[g], 32)
                    if g:
                        pool.wait_ge(half_ready, 2 * g)
                    nc.gpsimd.tensor_tensor(
                        rsin[:].rearrange("p t (a c) -> p t a c", a=2),
                        qk[:, g % 2].rearrange("p t (a c) -> p t a c", a=2),
                        sin_sb[:, g % 2].unsqueeze(2).to_broadcast([P, TG, 2, C]), ALU.mult).then_inc(sind, 1)

        @block.scalar
        def _(act):
            act.dma_start(id_sb[:], ident).then_inc(id_in, 16)
            act.dma_start(raw[:, a_of:a_of + WA], w_qkv).then_inc(wa_in, 16)
            act.dma_start(heads_sb[:], heads).then_inc(small_in, 16)
            act.dma_start(wp[:], w_proj).then_inc(small_in, 16)
            act.dma_start(bias[:], b_proj.partition_broadcast(P)).then_inc(small_in, 16)
            for s, o, n in ((wa_in, a_of, WA), (wf_in, f_of, WF), (wr_in, r_of, WR)):
                act.wait_ge(s, 16)
                nc.scalar.copy(wh[:, o:o + n], raw[:, o:o + n]).then_inc(w_hi, 1)
            for step in plan:
                if step[0] == "norm" and NORM_ON_ACT[step[1]]:
                    n, g = step[1:]
                    lane, j = lane_job(n, g)
                    act.wait_ge(nmr_ready[n], g + 1)
                    if j >= 2:
                        act.wait_ge(xT_ready[lane], j - 1)
                    for t in range(TG):
                        last = nc.scalar.activation(
                            xn[lane][:, j % 2, t, :], xs[:, TG * g + t, :], ACT.Identity,
                            bias=nmr[:, n, TG * g + t:TG * g + t + 1], scale=rstd[:, n, TG * g + t:TG * g + t + 1])
                    last.then_inc(xn_ready[n], 1)
                elif step[0] == "turn":
                    lane, j = lane_job(*step[1:])
                    bank = (MB, H1)[j % 2] if step[1] == 0 else MB
                    act.wait_ge(xT_ready[lane], j + 1)
                    lane_used(act, lane, j)
                    nc.scalar.copy(xh[lane][:, j % 2, :], bank[:]).then_inc(hi_ready[lane], 1)
                elif step[0] == "q":
                    g = step[1]
                    act.wait_ge(q_ready, g + 1)
                    if g >= 2:
                        act.wait_ge(qphi_ready, g - 1)
                    nc.scalar.activation(ebuf[:, g % 2, :], O[:], ACT.Exp).then_inc(eq_ready, 1)
                    nc.scalar.activation(rbuf[:, g % 2, :], O[:], ACT.Relu).then_inc(rq_ready, 1)
                elif step[0] == "kv":
                    g = step[1]
                    for pr in range(2):
                        n = 2 * g + pr
                        bank = ((S0, S1), (P0, P1))[g % 2][pr][:].rearrange("p (t c) -> p t c", t=2)
                        act.wait_ge(kv_ready, n + 1)
                        if n >= 2:
                            act.wait_ge(kphi_ready, n - 1)
                        nc.scalar.activation(ek[:, pr], bank[:, :, 0:C], ACT.Exp).then_inc(ek_ready, 1)
                        nc.scalar.activation(rk[:, pr], bank[:, :, 0:C], ACT.Relu).then_inc(rk_ready, 1)
                        nc.scalar.copy(vone[:, 2 * n:2 * n + 2, 0:C], bank[:, :, C:2 * C]).then_inc(vone_ready, 1)
                elif step[0] == "at":
                    g = step[1]
                    act.wait_ge(aT_ready, g + 1)
                    if g >= 2:
                        act.wait_ge(pr_ready, g - 1)
                    nc.scalar.copy(rbuf[:, g % 2, :], O[:]).then_inc(aTs_ready, 1)
                elif step[0] == "f1":
                    j = step[1]

                    def square(m):
                        n = M * j + m
                        act.wait_ge(relu_ready, n + 1)
                        if j >= 2:
                            act.wait_ge(y_ready, j - 1)
                        if n == 0:
                            act.wait_ge(w_lo, 3)
                        nc.scalar.activation(hid[:, j % 2, m, :], relu[:, n % 2, :], ACT.Square).then_inc(sq_ready, 1)

                    for m in range(M):
                        n = M * j + m
                        act.wait_ge(h_ready, n + 1)
                        if n >= 2:
                            act.wait_ge(sq_ready, n - 1)
                        nc.scalar.activation(relu[:, n % 2, :], (H0, H1)[m % 2][:], ACT.Relu).then_inc(relu_ready, 1)
                        if m:
                            square(m - 1)
                    square(M - 1)
                elif step[0] == "f2":
                    j = step[1]
                    act.wait_ge(y_ready, j + 1)
                    if j >= 2:
                        act.wait_ge(xf_ready, j - 1)
                    nc.scalar.copy(y[:, j % 2, :], MB[:]).then_inc(ysb_ready, 1)
                elif step[0] == "spike":
                    j = step[1]
                    if j == 0:
                        act.wait_ge(consts, 1)
                    else:
                        act.wait_ge(count_ready, j)
                    act.wait_ge(ysb_ready, j + 1)
                    for k in range(STEPS):
                        if k:
                            act.wait_ge(mem_ready, 2 * (STEPS - 1) * j + 2 * k)
                        src = y[:, j % 2, :] if k == 0 else mem[:, (k - 1) % 2, :]
                        nc.scalar.activation(sign[:, k, :], src, ACT.Sign, bias=above[:, 0:1],
                                             scale=JUST_BELOW_1 if k == 0 else -JUST_BELOW_1).then_inc(sign_ready, 1)
                elif step[0] == "qkv":
                    g = step[1]
                    if g >= 2:
                        act.wait_ge(cosd, g - 1)
                        act.wait_ge(sind, g - 1)
                    for t in range(TG):
                        n = TG * g + t
                        bank = (S0, S1)[n % 2]
                        act.wait_ge(qkv_ready, n + 1)
                        nc.scalar.copy(qk[:, g % 2, t, :], bank[:, 0:2 * C])
                        nc.scalar.copy(v[:, n, :], bank[:, 2 * C:3 * C]).then_inc(v_ready, 1)
                elif step[0] == "tqk":
                    g = step[1]
                    for k, (dst, bank) in enumerate(((qh, P0), (kh, P1))):
                        act.wait_ge(tqk_ready, 2 * g + k + 1)
                        nc.scalar.copy(dst[:, W * g:W * g + W], bank[:]).then_inc(qkhi_ready, 1)
                elif step[0] == "e":
                    i = step[1]
                    act.wait_ge(m_ready, i + 1)
                    for p, (a, b) in enumerate(exp_pieces(i)):
                        s = scores[i % 2]
                        nc.scalar.activation(s[:, a:b], s[:, a:b], ACT.Exp, bias=negm[:, i:i + 1], scale=1.0,
                                             accum_out=psums[:, i, p:p + 1]).then_inc(e_ready, 1)
                elif step[0] == "t":
                    i, jg = step[1:]
                    n = turn_no[i, jg]
                    nb = min(TG, i + 1 - TG * jg)
                    act.wait_ge(pt_ready, n + 1)
                    if n >= 3:
                        act.wait_ge(pv_ready, n - 2)
                    nc.scalar.copy(pt[:, n % 3, 0:P * nb], (P0, P1)[n % 2][:, 0:P * nb]).then_inc(ptc_ready, 1)

        @block.vector
        def _(dve):
            nc.vector.memset(vone[:, :, C:C + 1], 1.0).then_inc(vone_set, 1)
            lows = iter(((a_of, WA), (f_of, WF), (r_of, WR)))
            low_no = [0]

            def weight_low():
                o, n = next(lows)
                low_no[0] += 1
                dve.wait_ge(w_hi, low_no[0])
                nc.vector.tensor_tensor(wl[:, o:o + n], raw[:, o:o + n], wh[:, o:o + n], ALU.subtract).then_inc(w_lo, 1)

            for step in plan:
                if step[0] == "stats":
                    n, g = step[1:]
                    if n == 0:
                        dve.wait_ge(x_in[g], 16)
                    elif n == 1:
                        dve.wait_ge(x1_ready, g + 1)
                    elif n == 2:
                        dve.wait_ge(xf_ready, g + 1)
                    else:
                        dve.wait_ge(x3_ready, TG * (g + 1))
                    for t in range(TG * g, TG * g + TG):
                        last = nc.vector.bn_stats(stat[:, n, t, :], xs[:, t, :])
                    last.then_inc(bn_done[n], 1)
                    dve.wait_ge(bn_done[n], g + 1)
                    for t in range(TG * g, TG * g + TG):
                        last = nc.vector.bn_aggr(mom[:, n, t, :], stat[:, n, t, :])
                    last.then_inc(mom_ready[n], 1)
                    if n == 0 and g in (0,):
                        weight_low()
                elif step[0] == "norm" and not NORM_ON_ACT[step[1]]:
                    n, g = step[1:]
                    lane, j = lane_job(n, g)
                    dve.wait_ge(rstd_ready[n], g + 1)
                    if j >= 2:
                        dve.wait_ge(xT_ready[lane], j - 1)
                    for t in range(TG):
                        k = TG * g + t
                        last = nc.vector.tensor_scalar(xn[lane][:, j % 2, t, :], xs[:, k, :], mom[:, n, k, 0:1],
                                                       rstd[:, n, k:k + 1], ALU.subtract, ALU.mult)
                    last.then_inc(xn_ready[n], 1)
                elif step[0] == "turn":
                    lane, j = lane_job(*step[1:])
                    bank = (MB, H1)[j % 2] if step[1] == 0 else MB
                    dve.wait_ge(hi_ready[lane], j + 1)
                    nc.vector.tensor_tensor(xl[lane][:, j % 2, :], bank[:], xh[lane][:, j % 2, :],
                                            ALU.subtract).then_inc(lo_ready[lane], 1)
                elif step[0] == "q":
                    g = step[1]
                    dve.wait_ge(rq_ready, g + 1)
                    nc.vector.scalar_tensor_tensor(
                        out=qphi[:, W * g:W * g + W], in0=ebuf[:, g % 2, :], scalar=1.0, in1=rbuf[:, g % 2, :],
                        op0=ALU.min, op1=ALU.add).then_inc(qphi_ready, 1)
                elif step[0] == "kv":
                    g = step[1]
                    for pr in range(2):
                        n = 2 * g + pr
                        dve.wait_ge(rk_ready, n + 1)
                        nc.vector.scalar_tensor_tensor(
                            out=kphi[:, 2 * C * n:2 * C * n + 2 * C].rearrange("p (t c) -> p t c", t=2),
                            in0=ek[:, pr], scalar=1.0, in1=rk[:, pr], op0=ALU.min, op1=ALU.add).then_inc(kphi_ready, 1)
                    if g in (1, 2):
                        weight_low()
                elif step[0] == "diag":
                    dve.wait_ge(small_in, 48)
                    dve.wait_ge(sum_ready, 1)
                    nc.vector.tensor_tensor(bdkv[:], H0[:, 0:C], heads_sb[:, 0:C], ALU.mult).then_inc(diag_ready, 1)
                    nc.vector.tensor_scalar(bdks[:], heads_sb[:, C:C + HEADS], H0[:, C:C + 1], None,
                                            ALU.mult).then_inc(diag_ready, 1)
                elif step[0] == "ao":
                    g = step[1]
                    dve.wait_ge(ao_ready, g + 1)
                    nc.vector.tensor_scalar(den[:], P1[:, 0:TG * HEADS], EPS_ATT, None, ALU.add).then_inc(den_ready, 1)
                    dve.wait_ge(den_ready, g + 1)
                    nc.vector.reciprocal(rec[:], den[:]).then_inc(rec_ready, 1)
                    dve.wait_ge(rec_ready, g + 1)
                    if g >= 2:
                        dve.wait_ge(aT_ready, g - 1)
                    nc.vector.tensor_tensor(
                        ebuf[:, g % 2, :].rearrange("p (h d) -> p h d", d=HD),
                        P0[:].rearrange("p (h d) -> p h d", d=HD),
                        rec[:].unsqueeze(2).to_broadcast([P, TG * HEADS, HD]), ALU.mult).then_inc(heads_ready, 1)
                elif step[0] == "pr":
                    g = step[1]
                    dve.wait_ge(pr_ready, g + 1)
                    dve.wait_ge(xb_ready, g + 1)
                    xg = xs[:, TG * g:TG * g + TG, :].rearrange("p t c -> p (t c)")
                    nc.vector.tensor_tensor(xg, P1[:], xg, ALU.add).then_inc(x1_ready, 1)
                elif step[0] == "spike":
                    j = step[1]
                    ys = y[:, j % 2, :]
                    dve.wait_ge(ysb_ready, j + 1)
                    n = 2 * (STEPS - 1) * j
                    for k in range(STEPS - 1):
                        old = ys if k == 0 else mem[:, (k - 1) % 2, :]
                        sgn = 1.0 if k == 0 else -1.0
                        if n:
                            dve.wait_ge(mem_ready, n)
                        nc.vector.scalar_tensor_tensor(out=u[:], in0=old, scalar=sgn * BETA, in1=ys,
                                                       op0=ALU.mult, op1=ALU.add).then_inc(mem_ready, 1)
                        n += 1
                        dve.wait_ge(mem_ready, n)
                        if k >= 2:
                            dve.wait_ge(sign_ready, STEPS * j + k)
                        elif j:
                            dve.wait_ge(sign_ready, STEPS * (j - 1) + k + 4)
                        nc.vector.scalar_tensor_tensor(
                            out=mem[:, k % 2, :], in0=old, scalar=sgn * THRESHOLD, in1=u[:],
                            op0=ALU.is_gt if k == 0 else ALU.is_lt, op1=ALU.subtract).then_inc(mem_ready, 1)
                        n += 1
                elif step[0] == "count":
                    j = step[1]
                    g = j % G
                    dve.wait_ge(count_ready, j + 1)
                    xg = xs[:, TG * g:TG * g + TG, :].rearrange("p t c -> p (t c)")
                    nc.vector.scalar_tensor_tensor(out=xg, in0=H0[:], scalar=1.0 / STEPS, in1=xg,
                                                   op0=ALU.mult, op1=ALU.add).then_inc(xf_ready, 1)
                elif step[0] == "rope":
                    g = step[1]
                    dve.wait_ge(v_ready, TG * (g + 1))
                    dve.wait_ge(trig_in[g], 32)
                    if g >= 2:
                        dve.wait_ge(tqk_ready, 2 * (g - 1))
                    r = rot[:, g % 2].rearrange("p t (a c) -> p t a c", a=2)
                    nc.vector.tensor_tensor(
                        r, qk[:, g % 2].rearrange("p t (a c) -> p t a c", a=2),
                        cos_sb[:, g % 2].unsqueeze(2).to_broadcast([P, TG, 2, C]), ALU.mult).then_inc(cosd, 1)
                    dve.wait_ge(cosd, g + 1)
                    dve.wait_ge(sind, g + 1)
                    rr = rot[:, g % 2].rearrange("p t (a h c) -> p (t a) h c", a=2, h=2)
                    ss = rsin[:].rearrange("p t (a h c) -> p (t a) h c", a=2, h=2)
                    for h in range(2):
                        nc.vector.tensor_tensor(rr[:, :, h, :], rr[:, :, h, :], ss[:, :, 1 - h, :],
                                                ALU.add).then_inc(half_ready, 1)
                elif step[0] == "tqk":
                    g = step[1]
                    for k, (hi, lo, bank) in enumerate(((qh, ql, P0), (kh, kl, P1))):
                        dve.wait_ge(qkhi_ready, 2 * g + k + 1)
                        nc.vector.tensor_tensor(lo[:, W * g:W * g + W], bank[:], hi[:, W * g:W * g + W],
                                                ALU.subtract).then_inc(qklo_ready, 1)
                elif step[0] == "s":
                    i = step[1]
                    cuts = score_chunks(i)
                    if i >= 2:
                        dve.wait_ge(pt_ready, turn_no[i - 2, (i - 2) // TG] + 1)
                        dve.wait_ge(osb_ready, i - 1)
                    elif i == 0:
                        dve.wait_ge(mask_in, 16)
                        dve.wait_ge(ao_ready, G)
                    for c, (a, b) in enumerate(cuts):
                        n = chunk_no[i, c]
                        dve.wait_ge(s_ready, n + 1)
                        bank = (S0, S1)[n % 2][:, 0:b - a]
                        if c < len(cuts) - 1:
                            last = nc.vector.tensor_scalar(scores[i % 2][:, a:b], bank, SCALE, MASKED, ALU.mult,
                                                           ALU.max, accum_out=cmax[:, i, c:c + 1])
                        else:
                            m0 = MASK_LEAD - (P * i - a)
                            last = nc.vector.tensor_tensor_reduce(
                                scores[i % 2][:, a:b], bank, mask_sb[:, m0:m0 + b - a], SCALE, MASKED,
                                ALU.add, ALU.max, cmax[:, i, c:c + 1])
                        last.then_inc(sc_ready, 1)
                    dve.wait_ge(sc_ready, n + 1)
                    nc.vector.tensor_reduce(negm[:, i:i + 1], cmax[:, i, 0:len(cuts)], AX_X, ALU.max,
                                            negate=True).then_inc(m_ready, 1)
                elif step[0] == "o":
                    i = step[1]
                    np_ = len(exp_pieces(i))
                    dve.wait_ge(e_ready, piece_no[i, np_ - 1] + 1)
                    nc.vector.tensor_reduce(psum_all[:, i:i + 1], psums[:, i, 0:np_], AX_X, ALU.add).then_inc(ps_ready, 1)
                    dve.wait_ge(ps_ready, i + 1)
                    nc.vector.reciprocal(rsum[:, i:i + 1], psum_all[:, i:i + 1]).then_inc(rs_ready, 1)
                    dve.wait_ge(pv_ready, turn_no[i, i // TG] + 1)
                    o = O[:, C * (i % TG):C * (i % TG) + C]
                    if i < T - 1:
                        dve.wait_ge(vnext_in, 16 * ((i + 1) // TG + 1))
                        if i >= 2:
                            dve.wait_ge(x3_ready, i - 1)
                        nc.vector.scalar_tensor_tensor(
                            out=osb[:, i % 2, :], in0=vnext[:, i, :], scalar=scores[i % 2][:, P * (i + 1):P * (i + 1) + 1],
                            in1=o, op0=ALU.mult, op1=ALU.add).then_inc(osb_ready, 1)
                        dve.wait_ge(osb_ready, i + 1)
                        o = osb[:, i % 2, :]
                    dve.wait_ge(rs_ready, i + 1)
                    nc.vector.scalar_tensor_tensor(out=xs[:, i, :], in0=o, scalar=rsum[:, i:i + 1], in1=xs[:, i, :],
                                                   op0=ALU.mult, op1=ALU.add).then_inc(x3_ready, 1)

        @block.tensor
        def _(pe):
            reader = {}

            def claim(bank):
                if bank.name in reader:
                    pe.wait_ge(*reader[bank.name])

            def split_product(dst, stationary, moving):
                (sh, sl), (mh, ml) = stationary, moving
                nc.tensor.matmul(dst, sh, mh, start=True, stop=False)
                nc.tensor.matmul(dst, sh, ml, start=False, stop=False)
                return nc.tensor.matmul(dst, sl, mh, start=False, stop=True)

            for step in plan:
                if step[0] == "turn":
                    n, g = step[1:]
                    lane, j = lane_job(n, g)
                    bank = (MB, H1)[j % 2] if n == 0 else MB
                    if n == 0 and g == 0:
                        pe.wait_ge(id_in, 16)
                    pe.wait_ge(xn_ready[n], g + 1)
                    claim(bank)
                    for t in range(TG):
                        last = nc.tensor.transpose(bank[:, C * t:C * t + C], xn[lane][:, j % 2, t, :], id_sb[:])
                    last.then_inc(xT_ready[lane], 1)
                    reader[bank.name] = (lo_ready[lane], j + 1)
                elif step[0] == "q":
                    g = step[1]
                    pe.wait_ge(lo_ready[0], g + 1)
                    pe.wait_ge(w_lo, 1)
                    claim(O)
                    split_product(O[:], (wh[:, 0:C], wl[:, 0:C]),
                                  (xh[0][:, g % 2, :], xl[0][:, g % 2, :])).then_inc(q_ready, 1)
                    reader[O.name] = (rq_ready, g + 1)
                elif step[0] == "kv":
                    g = step[1]
                    for pr in range(2):
                        bank = ((S0, S1), (P0, P1))[g % 2][pr]
                        claim(bank)
                        for t in range(2):
                            o = C * (2 * pr + t)
                            last = split_product(
                                bank[:, 2 * C * t:2 * C * t + 2 * C],
                                (xh[0][:, g % 2, o:o + C], xl[0][:, g % 2, o:o + C]), (wh[:, C:3 * C], wl[:, C:3 * C]))
                        last.then_inc(kv_ready, 1)
                        reader[bank.name] = (vone_ready, 2 * g + pr + 1)
                elif step[0] == "acc":
                    g = step[1]
                    if g == 0:
                        pe.wait_ge(vone_set, 1)
                    pe.wait_ge(kphi_ready, 2 * g + 2)
                    pe.wait_ge(vone_ready, 2 * g + 2)
                    for t in range(TG * g, TG * g + TG):
                        last = nc.tensor.matmul(H0[:, 0:C + 1], kphi[:, C * t:C * t + C], vone[:, t, :],
                                                start=(t == 0), stop=(t == T - 1))
                    if g == G - 1:
                        last.then_inc(sum_ready, 1)
                        reader[H0.name] = (diag_ready, 2)
                elif step[0] == "ao":
                    g = step[1]
                    pe.wait_ge(diag_ready, 2)
                    pe.wait_ge(qphi_ready, g + 1)
                    claim(P0)
                    claim(P1)
                    for t in range(TG):
                        q_t = qphi[:, W * g + P * t:W * g + P * t + P]
                        nc.tensor.matmul(P0[:, C * t:C * t + C], q_t, bdkv[:], start=True, stop=True)
                        last = nc.tensor.matmul(P1[:, HEADS * t:HEADS * t + HEADS], q_t, bdks[:], start=True, stop=True)
                    last.then_inc(ao_ready, 1)
                    reader[P0.name] = reader[P1.name] = (heads_ready, g + 1)
                elif step[0] == "at":
                    g = step[1]
                    pe.wait_ge(heads_ready, g + 1)
                    claim(O)
                    for t in range(TG):
                        last = nc.tensor.transpose(O[:, C * t:C * t + C], ebuf[:, g % 2, C * t:C * t + C], id_sb[:])
                    last.then_inc(aT_ready, 1)
                    reader[O.name] = (aTs_ready, g + 1)
                elif step[0] == "pr":
                    g = step[1]
                    pe.wait_ge(aTs_ready, g + 1)
                    claim(P1)
                    for t in range(TG):
                        last = nc.tensor.matmul(P1[:, C * t:C * t + C], rbuf[:, g % 2, C * t:C * t + C], wp[:],
                                                start=True, stop=True)
                    last.then_inc(pr_ready, 1)
                    reader[P1.name] = (x1_ready, g + 1)
                elif step[0] == "f1":
                    j = step[1]
                    pe.wait_ge(w_lo, 2)
                    pe.wait_ge(lo_ready[1], j + 1)
                    for m in range(M):
                        bank = (H0, H1)[m % 2]
                        o = f_of + P * m
                        claim(bank)
                        split_product(bank[:], (wh[:, o:o + P], wl[:, o:o + P]),
                                      (xh[1][:, j % 2, :], xl[1][:, j % 2, :])).then_inc(h_ready, 1)
                        reader[bank.name] = (relu_ready, M * j + m + 1)
                elif step[0] == "f2":
                    j = step[1]
                    if j == 0:
                        pe.wait_ge(wd_in, 16)
                    pe.wait_ge(sq_ready, M * (j + 1))
                    claim(MB)
                    for t in range(TG):
                        for m in range(M):
                            last = nc.tensor.matmul(MB[:, C * t:C * t + C], hid[:, j % 2, m, P * t:P * t + P],
                                                    wd[:, m, :], start=(m == 0), stop=(m == M - 1))
                    last.then_inc(y_ready, 1)
                    reader[MB.name] = (ysb_ready, j + 1)
                elif step[0] == "count":
                    j = step[1]
                    pe.wait_ge(consts, 1)
                    claim(H0)
                    nc.tensor.matmul(H0[:], fives[:], ones[:], start=True, stop=False)
                    for k in range(STEPS):
                        pe.wait_ge(sign_ready, STEPS * j + k + 1)
                        last = nc.tensor.matmul(H0[:], half_id[:], sign[:, k, :], start=False, stop=(k == STEPS - 1))
                    last.then_inc(count_ready, 1)
                    reader[H0.name] = (xf_ready, j + 1)
                elif step[0] == "qkv":
                    g = step[1]
                    pe.wait_ge(w_lo, 3)
                    pe.wait_ge(lo_ready[0], G + g + 1)
                    for t in range(TG):
                        n = TG * g + t
                        bank = (S0, S1)[n % 2]
                        claim(bank)
                        split_product(bank[:, 0:3 * C], (xh[0][:, g % 2, P * t:P * t + P], xl[0][:, g % 2, P * t:P * t + P]),
                                      (wh[:, r_of:r_of + WR], wl[:, r_of:r_of + WR])).then_inc(qkv_ready, 1)
                        reader[bank.name] = (v_ready, n + 1)
                elif step[0] == "tqk":
                    g = step[1]
                    pe.wait_ge(half_ready, 2 * g + 2)
                    for k, bank in enumerate((P0, P1)):
                        claim(bank)
                        for t in range(TG):
                            last = nc.tensor.transpose(bank[:, P * t:P * t + P], rot[:, g % 2, t, C * k:C * k + C], id_sb[:])
                        last.then_inc(tqk_ready, 1)
                        reader[bank.name] = (qklo_ready, 2 * g + k + 1)
                elif step[0] == "s":
                    i = step[1]
                    pe.wait_ge(qklo_ready, 2 * (min(i + 1, T - 1) // TG) + 2)
                    for c, (a, b) in enumerate(score_chunks(i)):
                        n = chunk_no[i, c]
                        bank = (S0, S1)[n % 2]
                        claim(bank)
                        split_product(bank[:, 0:b - a], (qh[:, P * i:P * i + P], ql[:, P * i:P * i + P]),
                                      (kh[:, a:b], kl[:, a:b])).then_inc(s_ready, 1)
                        reader[bank.name] = (sc_ready, n + 1)
                elif step[0] == "t":
                    i, jg = step[1:]
                    n = turn_no[i, jg]
                    nb = min(TG, i + 1 - TG * jg)
                    end = P * (TG * jg + nb)
                    piece = next(p for p, (a, b) in enumerate(exp_pieces(i)) if end <= b)
                    bank = (P0, P1)[n % 2]
                    pe.wait_ge(e_ready, piece_no[i, piece] + 1)
                    claim(bank)
                    for b in range(nb):
                        k0 = P * (TG * jg + b)
                        last = nc.tensor.transpose(bank[:, P * b:P * b + P], scores[i % 2][:, k0:k0 + P], id_sb[:])
                    last.then_inc(pt_ready, 1)
                    reader[bank.name] = (ptc_ready, n + 1)
                elif step[0] == "pv":
                    i, jg = step[1:]
                    n = turn_no[i, jg]
                    nb = min(TG, i + 1 - TG * jg)
                    pe.wait_ge(ptc_ready, n + 1)
                    if jg == 0:
                        claim(O)
                    for b in range(nb):
                        k = TG * jg + b
                        last = nc.tensor.matmul(O[:, C * (i % TG):C * (i % TG) + C], pt[:, n % 3, P * b:P * b + P],
                                                v[:, k, :], start=(k == 0), stop=(k == i))
                    last.then_inc(pv_ready, 1)
                    if k == i:
                        reader[O.name] = (x3_ready, i + 1)


def rotary_tables():
    i = np.arange(HALF, dtype=np.float32)
    theta = np.power(np.float32(10000.0), np.float32(-2.0) * i / np.float32(C)).astype(np.float32)
    ang = np.arange(N_TOK, dtype=np.float32)[:, None] * theta[None, :]
    c, s = np.cos(ang), np.sin(ang)
    return np.concatenate([c, c], 1), np.concatenate([s, -s], 1)


def score_mask():
    q, k = np.arange(P)[:, None], np.arange(MASK_W)[None, :] - MASK_LEAD
    return np.where(k <= q + EXTRA, 0.0, MASKED).astype(np.float32)


def head_masks():
    own = (np.arange(C)[:, None] // HD == np.arange(C)[None, :] // HD)
    per = (np.arange(C)[:, None] // HD == np.arange(HEADS)[None, :])
    return np.concatenate([own, per], 1).astype(np.float32)


def kernel(L0_attn_a_x, L0_attn_a_Wqkv, L0_attn_a_Wproj, L0_attn_a_bproj, L0_attn_b_Wq, L0_attn_b_Wk,
           L0_attn_b_Wv, L0_ffn_W_fc, L0_ffn_W_proj):
    import concourse.bacc as _bacc
    from concourse.bass_utils import run_bass_kernel_spmd as _run

    lay = np.ascontiguousarray
    order = np.concatenate([np.arange(0, C, 2), np.arange(1, C, 2)])
    rope_rows = np.concatenate([np.asarray(L0_attn_b_Wq)[order], np.asarray(L0_attn_b_Wk)[order],
                                np.asarray(L0_attn_b_Wv)])
    cos, sin = rotary_tables()
    arrays = {
        "x": lay(np.asarray(L0_attn_a_x).reshape(N_TOK, C)),
        "w_qkv": lay(np.asarray(L0_attn_a_Wqkv).T),
        "w_proj": lay(np.asarray(L0_attn_a_Wproj).T),
        "b_proj": lay(np.asarray(L0_attn_a_bproj)),
        "w_fc": lay(np.asarray(L0_ffn_W_fc).T),
        "w_down": lay(np.asarray(L0_ffn_W_proj).T.reshape(M, P, C).transpose(1, 0, 2).reshape(P, M * C)),
        "w_rope": lay(rope_rows.T),
        "cos": lay(cos.astype(np.float32)),
        "sin": lay(sin.astype(np.float32)),
        "ident": np.eye(P, dtype=np.float32),
        "mask": score_mask(),
        "heads": head_masks(),
    }
    nc = _bacc.Bacc("TRN2", target_bir_lowering=False, num_devices=1)
    args = [nc.dram_tensor(f"in_{n}", a.shape, mybir.dt.from_np(a.dtype), kind="ExternalInput").ap()
            for n, a in arrays.items()]
    args.append(nc.dram_tensor("out_x", (N_TOK, C), F32, kind="ExternalOutput").ap())
    hybrid_block(nc, *args)
    r = _run(nc, [{f"in_{n}": a for n, a in arrays.items()}], core_ids=[0])
    return r.results[0]["out_x"].reshape(1, N_TOK, C)
```

```python
from contextlib import ExitStack

import numpy as np

import concourse.bass as bass
from concourse import mybir

F32 = mybir.dt.float32
F32R = mybir.dt.float32r
BF16 = mybir.dt.bfloat16
ALU = mybir.AluOpType
ACT = mybir.ActivationFunctionType
AX_X = mybir.AxisListType.X

P = 128
C = 128
N_TOK = 2048
T = N_TOK // P
TG = 4
G = T // TG
W = TG * P
HEADS = 16
HD = C // HEADS
F = 512
M = F // P
HALF = C // 2
EPS_LN = 1e-5
EPS_ATT = 1e-6
SCALE = float(1.0 / np.sqrt(np.float32(C)))
BETA, THRESHOLD, STEPS = 0.9, 1.0, 5
MASKED = -3.0e38
EXTRA = 1
MASK_LEAD = W - P
MASK_W = MASK_LEAD + 2 * P
EXP_PIECE = 1024
POOL_SQUARES = (1, 3)
JUST_BELOW_1 = 1.0 - 2.0 ** -24


def score_chunks(i):
    width = N_TOK if i == T - 1 else max(256, P * (i + 1) + 2 * EXTRA)
    cuts, at = [], 0
    while width - at > W:
        step = W if width - at - W >= 256 else width - at - 256
        cuts.append((at, at + step))
        at += step
    cuts.append((at, width))
    return cuts


def exp_pieces(i):
    width = score_chunks(i)[-1][1]
    return [(a, min(a + EXP_PIECE, width)) if width - a - EXP_PIECE > 256 else (a, width)
            for a in range(0, width, EXP_PIECE) if a == 0 or width - (a - EXP_PIECE) - EXP_PIECE > 256]


PLAN = """
stats-0-0 stats-0-1 stats-0-2 norm-0-0 norm-0-1 turn-0-0 stats-0-3 norm-0-2 turn-0-1 q-0 kv-0 norm-0-3 turn-0-2
kv-1 q-1 acc-0 turn-0-3 kv-2 kv-3 acc-1 q-2 acc-2 acc-3 bias-0 diag q-3 ao-0 at-0 pr-0 stats-1-0 bias-1 ao-1
at-1 pr-1 bias-2 stats-1-1 norm-1-0 turn-1-0 ao-2 f1-0-0 sq-0-0 f1-0-1 at-2 sq-0-1 norm-1-1 ao-3 f1-0-2 f1-0-3
turn-1-1 sq-0-2 at-3 pr-2 f1-1-0 sq-0-3 f2-0-0 sq-1-0 bias-3 f1-1-1 f1-1-2 sq-1-1 sq-1-2 f2-0-1 f1-1-3 sq-1-3
f2-0-2 f2-0-3 stats-1-2 spike-0-0 pr-3 f2-1-0 spike-0-1 norm-1-2 f2-1-1 f2-1-2 stats-1-3 spike-0-2 f2-1-3
turn-1-2 spike-0-3 f1-2-0 spike-0-4 f1-2-1 sq-2-0 count-0 norm-1-3 spike-1-0 f1-2-2 spike-1-1 turn-1-3 sq-2-1
f1-2-3 sq-2-2 sq-2-3 f1-3-0 stats-2-0 f2-2-0 f2-2-1 sq-3-0 spike-1-2 spike-1-3 f2-2-2 norm-2-0 f2-2-3 spike-1-4
f1-3-1 turn-2-0 count-1 stats-2-1 spike-2-0 qkv-0 spike-2-1 norm-2-1 spike-2-2 turn-2-1 rope-0 spike-2-3 f1-3-2
sq-3-1 f1-3-3 qkv-1 spike-2-4 tqk-0 count-2 sq-3-2 s-0-0 sq-3-3 rope-1 stats-2-2 f2-3-0 f2-3-1 s-1-0 e-0 f2-3-2
t-0-0 f2-3-3 spike-3-0 e-1 t-1-0 norm-2-2 pv-0-0 o-0 s-2-0 spike-3-1 pv-1-0 turn-2-2 e-2 spike-3-2 tqk-1 qkv-2
t-2-0 o-1 spike-3-3 s-3-0 s-3-1 pv-2-0 o-2 spike-3-4 s-4-0 s-4-1 e-3 count-3 t-3-0 stats-2-3 pv-3-0 e-4 t-4-0
o-3 stats-3-0 t-4-1 norm-2-3 pv-4-0 turn-2-3 norm-3-0 pv-4-1 s-5-0 rope-2 turn-3-0 qkv-3 f1-4-0 o-4 s-5-1 tqk-2
s-6-0 e-5 sq-4-0 f1-4-1 s-6-1 rope-3 t-5-0 e-6 f1-4-2 t-5-1 sq-4-1 f1-4-3 sq-4-2 pv-5-0 sq-4-3 t-6-0 pv-5-1 o-5
t-6-1 s-7-0 pv-6-0 s-7-1 f2-4-0 pv-6-1 o-6 s-7-2 e-7 f2-4-1 s-8-0 s-8-1 f2-4-2 s-8-2 t-7-0 t-7-1 e-8 f2-4-3
pv-7-0 pv-7-1 t-8-0 o-7 stats-3-1 s-9-0 t-8-1 t-8-2 s-9-1 tqk-3 norm-3-1 s-9-2 spike-4-0 pv-8-0 pv-8-1 turn-3-1
pv-8-2 o-8 s-10-0 e-9 f1-5-0 spike-4-1 s-10-1 sq-5-0 t-9-0 f1-5-1 t-9-1 sq-5-1 spike-4-2 f1-5-2 s-10-2 pv-9-0
f1-5-3 t-9-2 spike-4-3 pv-9-1 sq-5-2 sq-5-3 spike-4-4 pv-9-2 o-9 s-11-0 s-11-1 e-10 count-4 store-0 t-10-0
t-10-1 f2-5-0 pv-10-0 t-10-2 f2-5-1 pv-10-1 s-11-2 s-11-3 f2-5-2 pv-10-2 e-11 f2-5-3 o-10 spike-5-0 t-11-0
s-12-0 s-12-1 t-11-1 pv-11-0 s-12-2 s-12-3 t-11-2 pv-11-1 pv-11-2 spike-5-1 e-12 o-11 t-12-0 stats-3-2 spike-5-2
t-12-1 s-13-0 pv-12-0 s-13-1 pv-12-1 s-13-2 norm-3-2 t-12-2 t-12-3 s-13-3 turn-3-2 e-13 pv-12-2 pv-12-3 o-12
s-14-0 f1-6-0 f1-6-1 sq-6-0 t-13-0 s-14-1 t-13-1 f1-6-2 pv-13-0 t-13-2 sq-6-1 f1-6-3 pv-13-1 s-14-2 sq-6-2
sq-6-3 t-13-3 s-14-3 f2-6-0 pv-13-2 pv-13-3 e-14 o-13 spike-5-3 f2-6-1 t-14-0 spike-5-4 f2-6-2 s-15-0 pv-14-0
count-5 store-1 s-15-1 t-14-1 s-15-2 s-15-3 f2-6-3 spike-6-0 pv-14-1 t-14-2 t-14-3 pv-14-2 e-15 pv-14-3 o-14
t-15-0 t-15-1 pv-15-0 spike-6-1 spike-6-2 t-15-2 pv-15-1 spike-6-3 t-15-3 spike-6-4 pv-15-2 pv-15-3 o-15
stats-3-3 norm-3-3 count-6 store-2 turn-3-3 f1-7-0 f1-7-1 sq-7-0 f1-7-2 sq-7-1 f1-7-3 sq-7-2 sq-7-3 f2-7-0
f2-7-1 f2-7-2 f2-7-3 spike-7-0 spike-7-1 spike-7-2 spike-7-3 spike-7-4 count-7 store-3
"""


def make_plan():
    return [(name, *map(int, rest)) for name, *rest in (word.split("-") for word in PLAN.split())]


def hybrid_block(nc, x, w_qkv, w_proj, b_proj, w_fc, w_down, w_rope, cos, sin, ident, mask, heads, out):
    plan = make_plan()
    chunk_no, piece_no, turn_no = {}, {}, {}
    for step in plan:
        if step[0] == "s":
            chunk_no[step[1:]] = len(chunk_no)
        if step[0] == "e":
            for p in range(len(exp_pieces(step[1]))):
                piece_no[step[1], p] = len(piece_no)
        if step[0] == "t":
            turn_no[step[1:]] = len(turn_no)

    with ExitStack() as ctx:
        def sb(name, *shape, dt=F32):
            return ctx.enter_context(nc.sbuf_tensor(name, [P, *shape], dt))

        def sem(name):
            return ctx.enter_context(nc.semaphore(name))

        def sems(name, n):
            return [sem(f"{name}{i}") for i in range(n)]

        S0, S1, P0, P1, O, H0, H1, MB = (
            ctx.enter_context(nc.psum_tensor(f"bank_{n}", [P, W], F32))
            for n in ("s0", "s1", "p0", "p1", "o", "h0", "h1", "m"))

        xs = sb("xs", T, C)
        stat = sb("stat", 4, T, 6)
        mom = sb("mom", 4, T, 2)
        veps = sb("veps", 4, T)
        rstd = sb("rstd", 4, T)
        nmean = sb("nmean", 4, T)
        nmr = sb("nmr", 4, T)
        mhalf = sb("mhalf", TG)
        xn = [sb(f"xn{k}", 2, TG, C) for k in range(2)]
        xh = [sb(f"xh{k}", 2, W, dt=F32R) for k in range(2)]
        xl = [sb(f"xl{k}", 2, W, dt=F32R) for k in range(2)]
        ebuf = sb("ebuf", 2, W)
        rbuf = sb("rbuf", 2, W)
        qphi = sb("qphi", N_TOK)
        kphi = sb("kphi", N_TOK)
        vone = sb("vone", T, C + 1)
        bdkv = sb("bdkv", C)
        bdks = sb("bdks", HEADS)
        den = sb("den", TG * HEADS)
        rec = sb("rec", TG * HEADS)
        relu = sb("relu", 2, W)
        ek, rk = (relu[:, k, :].rearrange("p (r t c) -> p r t c", r=2, t=2) for k in range(2))
        hid = sb("hid", 2, M, W)
        y = sb("y", 2, W)
        u = sb("u", W)
        mem = sb("mem", 2, W)
        sign = sb("sign", STEPS, W, dt=BF16)
        half_id = sb("half_id", P, dt=BF16)
        fives = sb("fives", P, dt=BF16)
        ones = sb("ones", W, dt=BF16)
        above = sb("above", 1)
        qk = sb("qk", 2, TG, 2 * C)
        rot = sb("rot", 2, TG, 2 * C)
        rsin = sb("rsin", TG, 2 * C)
        cos_sb = sb("cos_sb", 2, TG, C)
        sin_sb = sb("sin_sb", 2, TG, C)
        qh, ql, kh, kl = (sb(n, N_TOK, dt=F32R) for n in ("qh", "ql", "kh", "kl"))
        v = sb("v", T, C)
        vnext = sb("vnext", T, C)
        cmax = sb("cmax", T, 4)
        negm = sb("negm", T)
        psums = sb("psums", T, 2)
        psum_all = sb("psum_all", T)
        rsum = sb("rsum", T)
        pt = sb("pt", 3, W)
        osb = sb("osb", 2, C)
        WA, WF, WR = 3 * C, F, 3 * C
        wh = sb("wh", WA + WF + WR, dt=F32R)
        wl = sb("wl", WA + WF + WR, dt=F32R)
        wp = sb("wp", C)
        wd = sb("wd", M, C)
        bias = sb("bias", C)
        id_sb = sb("id_sb", P)
        mask_sb = sb("mask_sb", MASK_W)
        heads_sb = sb("heads_sb", C + HEADS)
        raw = hid[:].rearrange("p a m w -> p (a m w)")[:, 0:WA + WF + WR]
        a_of, f_of, r_of = 0, WA, WA + WF
        scores = [qphi, kphi]

        x_in = sems("x_in", G)
        wa_in, wf_in, wr_in, id_in, small_in, wd_in, mask_in = (
            sem(n) for n in ("wa_in", "wf_in", "wr_in", "id_in", "small_in", "wd_in", "mask_in"))
        trig_in = sems("trig_in", G)
        vnext_in, stored = sems("vnext_in", G), sem("stored")
        w_hi, w_lo, consts = sem("w_hi"), sem("w_lo"), sem("consts")
        vnext_zero, vone_set = sem("vnext_zero"), sem("vone_set")
        bn_done, mom_ready, veps_ready, rstd_ready, nmr_ready, xn_ready = (
            sems(n, 4) for n in ("bn_done", "mom_ready", "veps_ready", "rstd_ready", "nmr_ready", "xn_ready"))
        xT_ready, hi_ready, lo_ready = (sems(n, 2) for n in ("xT_ready", "hi_ready", "lo_ready"))
        (q_ready, eq_ready, rq_ready, qphi_ready, kv_ready, ek_ready, rk_ready, vone_ready, kphi_ready, sum_ready,
         diag_ready, ao_ready, den_ready, rec_ready, heads_ready, aT_ready, aTs_ready, pr_ready, xb_ready,
         x1_ready) = (sem(n) for n in (
             "q_ready", "eq_ready", "rq_ready", "qphi_ready", "kv_ready", "ek_ready", "rk_ready", "vone_ready",
             "kphi_ready", "sum_ready", "diag_ready", "ao_ready", "den_ready", "rec_ready", "heads_ready",
             "aT_ready", "aTs_ready", "pr_ready", "xb_ready", "x1_ready"))
        h_ready, relu_ready, sq_ready, sqp_ready, y_ready, ysb_ready, mem_ready, sign_ready, count_ready, xf_ready = (
            sem(n) for n in ("h_ready", "relu_ready", "sq_ready", "sqp_ready", "y_ready", "ysb_ready", "mem_ready",
                             "sign_ready", "count_ready", "xf_ready"))
        (qkv_ready, v_ready, cosd, sind, half_ready, tqk_ready, qkhi_ready, qklo_ready, s_ready, sc_ready,
         m_ready, e_ready, pt_ready, ptc_ready, pv_ready, ps_ready, rs_ready, osb_ready, x3_ready) = (
             sem(n) for n in (
                 "qkv_ready", "v_ready", "cosd", "sind", "half_ready", "tqk_ready", "qkhi_ready", "qklo_ready",
                 "s_ready", "sc_ready", "m_ready", "e_ready", "pt_ready", "ptc_ready", "pv_ready",
                 "ps_ready", "rs_ready", "osb_ready", "x3_ready"))

        NORM_ON_ACT = (False, True, True, True)

        def lane_job(norm, g):
            return norm % 2, G * (norm // 2) + g

        def lane_used(eng, lane, j):
            if j < 2:
                return
            if lane == 1:
                eng.wait_ge(h_ready, M * (j - 1))
            elif j - 2 < G:
                eng.wait_ge(kv_ready, 2 * (j - 1))
            else:
                eng.wait_ge(qkv_ready, TG * (j - 1 - G))

        def on_pool(m):
            return m in POOL_SQUARES

        def squared(n):
            j, m = divmod(n, M)
            same = [k for k in range(M) if on_pool(k) == on_pool(m)]
            return (sqp_ready if on_pool(m) else sq_ready), len(same) * j + same.index(m) + 1

        block = ctx.enter_context(nc.Block())

        @block.sync
        def _(sp):
            x_t = x.rearrange("(t p) c -> p t c", p=P)
            o_t = out.rearrange("(t p) c -> p t c", p=P)
            for g in range(G):
                sp.dma_start(xs[:, TG * g:TG * g + TG, :], x_t[:, TG * g:TG * g + TG, :]).then_inc(x_in[g], 16)
            sp.dma_start(wd[:].rearrange("p m c -> p (m c)"), w_down).then_inc(wd_in, 16)
            for step in plan:
                if step[0] == "norm" and step[1] == 2:
                    g = step[2]
                    if g >= 2:
                        sp.wait_ge(cosd, g - 1)
                        sp.wait_ge(sind, g - 1)
                    for dst, src in ((cos_sb, cos), (sin_sb, sin)):
                        sp.dma_start(dst[:, g % 2], src.rearrange("(t p) c -> p t c", p=P)[
                            :, TG * g:TG * g + TG, :]).then_inc(trig_in[g], 16)
                if step[0] == "rope":
                    g = step[1]
                    sp.wait_ge(v_ready, TG * (g + 1))
                    sp.wait_ge(vnext_zero, 1)
                    a = max(1, TG * g)
                    sp.dma_start(vnext[P - 1:P, a - 1:TG * g + TG - 1, :],
                                 v[0:1, a:TG * g + TG, :]).then_inc(vnext_in[g], 16)
                if step[0] == "store":
                    g = step[1]
                    sp.wait_ge(xf_ready, G + g + 1)
                    sp.dma_start(o_t[:, TG * g:TG * g + TG, :], xs[:, TG * g:TG * g + TG, :]).then_inc(stored, 16)
            sp.wait_ge(stored, 16 * G)

        @block.gpsimd
        def _(pool):
            pool.dma_start(raw[:, f_of:f_of + WF], w_fc).then_inc(wf_in, 16)
            pool.dma_start(raw[:, r_of:r_of + WR], w_rope).then_inc(wr_in, 16)
            pool.dma_start(mask_sb[:], mask).then_inc(mask_in, 16)
            nc.gpsimd.memset(mhalf[:], -0.5)
            nc.gpsimd.memset(above[:], -1.0)
            nc.gpsimd.memset(fives[:], STEPS / 2 / P)
            nc.gpsimd.memset(ones[:], 1.0)
            pool.wait_ge(id_in, 16)
            nc.gpsimd.tensor_scalar(half_id[:], id_sb[:], 0.5, None, ALU.mult).then_inc(consts, 1)
            for step in plan:
                if step[0] == "stats":
                    n, g = step[1:]
                    ts = slice(TG * g, TG * g + TG)
                    pool.wait_ge(mom_ready[n], g + 1)
                    nc.gpsimd.tensor_scalar_add(veps[:, n, ts], mom[:, n, ts, 1], EPS_LN).then_inc(veps_ready[n], 1)
                    nc.gpsimd.tensor_scalar(nmean[:, n, ts], mom[:, n, ts, 0], -1.0, None, ALU.mult).then_inc(
                        veps_ready[n], 1)
                    pool.wait_ge(veps_ready[n], 2 * (g + 1))
                    pool.wait_ge(consts, 1)
                    nc.gpsimd.tensor_tensor(rstd[:, n, ts], veps[:, n, ts], mhalf[:], ALU.pow).then_inc(rstd_ready[n], 1)
                    if NORM_ON_ACT[n]:
                        pool.wait_ge(rstd_ready[n], g + 1)
                        nc.gpsimd.tensor_tensor(nmr[:, n, ts], nmean[:, n, ts], rstd[:, n, ts],
                                                ALU.mult).then_inc(nmr_ready[n], 1)
                elif step[0] == "bias":
                    g = step[1]
                    pool.wait_ge(xn_ready[0], g + 1)
                    if g == 0:
                        pool.wait_ge(small_in, 48)
                    xg = xs[:, TG * g:TG * g + TG, :]
                    nc.gpsimd.tensor_tensor(xg, xg, bias[:].unsqueeze(1).to_broadcast([P, TG, C]),
                                            ALU.add).then_inc(xb_ready, 1)
                    if g == 0:
                        nc.gpsimd.memset(vnext[:], 0.0).then_inc(vnext_zero, 1)
                elif step[0] == "sq" and on_pool(step[2]):
                    j, m = step[1:]
                    n = M * j + m
                    pool.wait_ge(relu_ready, n + 1)
                    if j >= 2:
                        pool.wait_ge(y_ready, j - 1)
                    if j == 0:
                        pool.wait_ge(w_lo, 3)
                    r = relu[:, n % 2, :]
                    nc.gpsimd.tensor_tensor(hid[:, j % 2, m, :], r, r, ALU.mult).then_inc(sqp_ready, 1)
                elif step[0] == "rope":
                    g = step[1]
                    pool.wait_ge(v_ready, TG * (g + 1))
                    pool.wait_ge(trig_in[g], 32)
                    if g:
                        pool.wait_ge(half_ready, 2 * g)
                    nc.gpsimd.tensor_tensor(
                        rsin[:].rearrange("p t (a c) -> p t a c", a=2),
                        qk[:, g % 2].rearrange("p t (a c) -> p t a c", a=2),
                        sin_sb[:, g % 2].unsqueeze(2).to_broadcast([P, TG, 2, C]), ALU.mult).then_inc(sind, 1)

        @block.scalar
        def _(act):
            act.dma_start(id_sb[:], ident).then_inc(id_in, 16)
            act.dma_start(raw[:, a_of:a_of + WA], w_qkv).then_inc(wa_in, 16)
            act.dma_start(heads_sb[:], heads).then_inc(small_in, 16)
            act.dma_start(wp[:], w_proj).then_inc(small_in, 16)
            act.dma_start(bias[:], b_proj.partition_broadcast(P)).then_inc(small_in, 16)
            for s, o, n in ((wa_in, a_of, WA), (wf_in, f_of, WF), (wr_in, r_of, WR)):
                act.wait_ge(s, 16)
                nc.scalar.copy(wh[:, o:o + n], raw[:, o:o + n]).then_inc(w_hi, 1)
            for step in plan:
                if step[0] == "norm" and NORM_ON_ACT[step[1]]:
                    n, g = step[1:]
                    lane, j = lane_job(n, g)
                    act.wait_ge(nmr_ready[n], g + 1)
                    if j >= 2:
                        act.wait_ge(xT_ready[lane], j - 1)
                    for t in range(TG):
                        last = nc.scalar.activation(
                            xn[lane][:, j % 2, t, :], xs[:, TG * g + t, :], ACT.Identity,
                            bias=nmr[:, n, TG * g + t:TG * g + t + 1], scale=rstd[:, n, TG * g + t:TG * g + t + 1])
                    last.then_inc(xn_ready[n], 1)
                elif step[0] == "turn":
                    lane, j = lane_job(*step[1:])
                    bank = (MB, H1)[j % 2] if step[1] == 0 else MB
                    act.wait_ge(xT_ready[lane], j + 1)
                    lane_used(act, lane, j)
                    nc.scalar.copy(xh[lane][:, j % 2, :], bank[:]).then_inc(hi_ready[lane], 1)
                elif step[0] == "q":
                    g = step[1]
                    act.wait_ge(q_ready, g + 1)
                    if g >= 2:
                        act.wait_ge(qphi_ready, g - 1)
                    nc.scalar.activation(ebuf[:, g % 2, :], O[:], ACT.Exp).then_inc(eq_ready, 1)
                    nc.scalar.activation(rbuf[:, g % 2, :], O[:], ACT.Relu).then_inc(rq_ready, 1)
                elif step[0] == "kv":
                    g = step[1]
                    for pr in range(2):
                        n = 2 * g + pr
                        bank = ((S0, S1), (P0, P1))[g % 2][pr][:].rearrange("p (t c) -> p t c", t=2)
                        act.wait_ge(kv_ready, n + 1)
                        if n >= 2:
                            act.wait_ge(kphi_ready, n - 1)
                        nc.scalar.activation(ek[:, pr], bank[:, :, 0:C], ACT.Exp).then_inc(ek_ready, 1)
                        nc.scalar.activation(rk[:, pr], bank[:, :, 0:C], ACT.Relu).then_inc(rk_ready, 1)
                        nc.scalar.copy(vone[:, 2 * n:2 * n + 2, 0:C], bank[:, :, C:2 * C]).then_inc(vone_ready, 1)
                elif step[0] == "at":
                    g = step[1]
                    act.wait_ge(aT_ready, g + 1)
                    if g >= 2:
                        act.wait_ge(pr_ready, g - 1)
                    nc.scalar.copy(rbuf[:, g % 2, :], O[:]).then_inc(aTs_ready, 1)
                elif step[0] == "f1":
                    j, m = step[1:]
                    n = M * j + m
                    act.wait_ge(h_ready, n + 1)
                    if n >= 2:
                        act.wait_ge(*squared(n - 2))
                    nc.scalar.activation(relu[:, n % 2, :], (H0, H1)[m % 2][:], ACT.Relu).then_inc(relu_ready, 1)
                elif step[0] == "sq" and not on_pool(step[2]):
                    j, m = step[1:]
                    n = M * j + m
                    act.wait_ge(relu_ready, n + 1)
                    if j >= 2:
                        act.wait_ge(y_ready, j - 1)
                    if n == 0:
                        act.wait_ge(w_lo, 3)
                    nc.scalar.activation(hid[:, j % 2, m, :], relu[:, n % 2, :], ACT.Square).then_inc(sq_ready, 1)
                elif step[0] == "f2" and step[2] == TG - 1:
                    j = step[1]
                    act.wait_ge(y_ready, j + 1)
                    if j >= 2:
                        act.wait_ge(xf_ready, j - 1)
                    nc.scalar.copy(y[:, j % 2, :], MB[:]).then_inc(ysb_ready, 1)
                elif step[0] == "spike":
                    j, k = step[1:]
                    if k == 0:
                        if j == 0:
                            act.wait_ge(consts, 1)
                        else:
                            act.wait_ge(count_ready, j)
                        act.wait_ge(ysb_ready, j + 1)
                        src = y[:, j % 2, :]
                    else:
                        act.wait_ge(mem_ready, 2 * (STEPS - 1) * j + 2 * k)
                        src = mem[:, (k - 1) % 2, :]
                    nc.scalar.activation(sign[:, k, :], src, ACT.Sign, bias=above[:, 0:1],
                                         scale=JUST_BELOW_1 if k == 0 else -JUST_BELOW_1).then_inc(sign_ready, 1)
                elif step[0] == "qkv":
                    g = step[1]
                    if g >= 2:
                        act.wait_ge(cosd, g - 1)
                        act.wait_ge(sind, g - 1)
                    for t in range(TG):
                        n = TG * g + t
                        bank = (S0, S1)[n % 2]
                        act.wait_ge(qkv_ready, n + 1)
                        nc.scalar.copy(qk[:, g % 2, t, :], bank[:, 0:2 * C])
                        nc.scalar.copy(v[:, n, :], bank[:, 2 * C:3 * C]).then_inc(v_ready, 1)
                elif step[0] == "tqk":
                    g = step[1]
                    for k, (dst, bank) in enumerate(((qh, P0), (kh, P1))):
                        act.wait_ge(tqk_ready, 2 * g + k + 1)
                        nc.scalar.copy(dst[:, W * g:W * g + W], bank[:]).then_inc(qkhi_ready, 1)
                elif step[0] == "e":
                    i = step[1]
                    act.wait_ge(m_ready, i + 1)
                    for p, (a, b) in enumerate(exp_pieces(i)):
                        s = scores[i % 2]
                        nc.scalar.activation(s[:, a:b], s[:, a:b], ACT.Exp, bias=negm[:, i:i + 1], scale=1.0,
                                             accum_out=psums[:, i, p:p + 1]).then_inc(e_ready, 1)
                elif step[0] == "t":
                    i, jg = step[1:]
                    n = turn_no[i, jg]
                    nb = min(TG, i + 1 - TG * jg)
                    act.wait_ge(pt_ready, n + 1)
                    if n >= 3:
                        act.wait_ge(pv_ready, n - 2)
                    nc.scalar.copy(pt[:, n % 3, 0:P * nb], (P0, P1)[n % 2][:, 0:P * nb]).then_inc(ptc_ready, 1)

        @block.vector
        def _(dve):
            nc.vector.memset(vone[:, :, C:C + 1], 1.0).then_inc(vone_set, 1)
            lows = iter(((a_of, WA), (f_of, WF), (r_of, WR)))
            low_no = [0]

            def weight_low():
                o, n = next(lows)
                low_no[0] += 1
                dve.wait_ge(w_hi, low_no[0])
                nc.vector.tensor_tensor(wl[:, o:o + n], raw[:, o:o + n], wh[:, o:o + n], ALU.subtract).then_inc(w_lo, 1)

            for step in plan:
                if step[0] == "stats":
                    n, g = step[1:]
                    if n == 0:
                        dve.wait_ge(x_in[g], 16)
                    elif n == 1:
                        dve.wait_ge(x1_ready, g + 1)
                    elif n == 2:
                        dve.wait_ge(xf_ready, g + 1)
                    else:
                        dve.wait_ge(x3_ready, TG * (g + 1))
                    for t in range(TG * g, TG * g + TG):
                        last = nc.vector.bn_stats(stat[:, n, t, :], xs[:, t, :])
                    last.then_inc(bn_done[n], 1)
                    dve.wait_ge(bn_done[n], g + 1)
                    for t in range(TG * g, TG * g + TG):
                        last = nc.vector.bn_aggr(mom[:, n, t, :], stat[:, n, t, :])
                    last.then_inc(mom_ready[n], 1)
                    if n == 0 and g in (0,):
                        weight_low()
                elif step[0] == "norm" and not NORM_ON_ACT[step[1]]:
                    n, g = step[1:]
                    lane, j = lane_job(n, g)
                    dve.wait_ge(rstd_ready[n], g + 1)
                    if j >= 2:
                        dve.wait_ge(xT_ready[lane], j - 1)
                    for t in range(TG):
                        k = TG * g + t
                        last = nc.vector.tensor_scalar(xn[lane][:, j % 2, t, :], xs[:, k, :], mom[:, n, k, 0:1],
                                                       rstd[:, n, k:k + 1], ALU.subtract, ALU.mult)
                    last.then_inc(xn_ready[n], 1)
                elif step[0] == "turn":
                    lane, j = lane_job(*step[1:])
                    bank = (MB, H1)[j % 2] if step[1] == 0 else MB
                    dve.wait_ge(hi_ready[lane], j + 1)
                    nc.vector.tensor_tensor(xl[lane][:, j % 2, :], bank[:], xh[lane][:, j % 2, :],
                                            ALU.subtract).then_inc(lo_ready[lane], 1)
                elif step[0] == "q":
                    g = step[1]
                    dve.wait_ge(rq_ready, g + 1)
                    nc.vector.scalar_tensor_tensor(
                        out=qphi[:, W * g:W * g + W], in0=ebuf[:, g % 2, :], scalar=1.0, in1=rbuf[:, g % 2, :],
                        op0=ALU.min, op1=ALU.add).then_inc(qphi_ready, 1)
                elif step[0] == "kv":
                    g = step[1]
                    for pr in range(2):
                        n = 2 * g + pr
                        dve.wait_ge(rk_ready, n + 1)
                        nc.vector.scalar_tensor_tensor(
                            out=kphi[:, 2 * C * n:2 * C * n + 2 * C].rearrange("p (t c) -> p t c", t=2),
                            in0=ek[:, pr], scalar=1.0, in1=rk[:, pr], op0=ALU.min, op1=ALU.add).then_inc(kphi_ready, 1)
                    if g in (1, 2):
                        weight_low()
                elif step[0] == "diag":
                    dve.wait_ge(small_in, 48)
                    dve.wait_ge(sum_ready, 1)
                    nc.vector.tensor_tensor(bdkv[:], H0[:, 0:C], heads_sb[:, 0:C], ALU.mult).then_inc(diag_ready, 1)
                    nc.vector.tensor_scalar(bdks[:], heads_sb[:, C:C + HEADS], H0[:, C:C + 1], None,
                                            ALU.mult).then_inc(diag_ready, 1)
                elif step[0] == "ao":
                    g = step[1]
                    dve.wait_ge(ao_ready, g + 1)
                    nc.vector.tensor_scalar(den[:], P1[:, 0:TG * HEADS], EPS_ATT, None, ALU.add).then_inc(den_ready, 1)
                    dve.wait_ge(den_ready, g + 1)
                    nc.vector.reciprocal(rec[:], den[:]).then_inc(rec_ready, 1)
                    dve.wait_ge(rec_ready, g + 1)
                    if g >= 2:
                        dve.wait_ge(aT_ready, g - 1)
                    else:
                        dve.wait_ge(qphi_ready, G)
                    nc.vector.tensor_tensor(
                        ebuf[:, g % 2, :].rearrange("p (h d) -> p h d", d=HD),
                        P0[:].rearrange("p (h d) -> p h d", d=HD),
                        rec[:].unsqueeze(2).to_broadcast([P, TG * HEADS, HD]), ALU.mult).then_inc(heads_ready, 1)
                elif step[0] == "pr":
                    g = step[1]
                    dve.wait_ge(pr_ready, g + 1)
                    dve.wait_ge(xb_ready, g + 1)
                    xg = xs[:, TG * g:TG * g + TG, :].rearrange("p t c -> p (t c)")
                    nc.vector.tensor_tensor(xg, P1[:], xg, ALU.add).then_inc(x1_ready, 1)
                elif step[0] == "spike":
                    j, k = step[1:]
                    if k == STEPS - 1:
                        continue
                    ys = y[:, j % 2, :]
                    n = 2 * (STEPS - 1) * j + 2 * k
                    old, sgn = (ys, 1.0) if k == 0 else (mem[:, (k - 1) % 2, :], -1.0)
                    if k == 0:
                        dve.wait_ge(ysb_ready, j + 1)
                    if n:
                        dve.wait_ge(mem_ready, n)
                    nc.vector.scalar_tensor_tensor(out=u[:], in0=old, scalar=sgn * BETA, in1=ys,
                                                   op0=ALU.mult, op1=ALU.add).then_inc(mem_ready, 1)
                    dve.wait_ge(mem_ready, n + 1)
                    if k >= 2:
                        dve.wait_ge(sign_ready, STEPS * j + k)
                    elif j:
                        dve.wait_ge(sign_ready, STEPS * (j - 1) + k + 4)
                    nc.vector.scalar_tensor_tensor(
                        out=mem[:, k % 2, :], in0=old, scalar=sgn * THRESHOLD, in1=u[:],
                        op0=ALU.is_gt if k == 0 else ALU.is_lt, op1=ALU.subtract).then_inc(mem_ready, 1)
                elif step[0] == "count":
                    j = step[1]
                    g = j % G
                    dve.wait_ge(count_ready, j + 1)
                    xg = xs[:, TG * g:TG * g + TG, :].rearrange("p t c -> p (t c)")
                    nc.vector.scalar_tensor_tensor(out=xg, in0=H0[:], scalar=1.0 / STEPS, in1=xg,
                                                   op0=ALU.mult, op1=ALU.add).then_inc(xf_ready, 1)
                elif step[0] == "rope":
                    g = step[1]
                    dve.wait_ge(v_ready, TG * (g + 1))
                    dve.wait_ge(trig_in[g], 32)
                    if g >= 2:
                        dve.wait_ge(tqk_ready, 2 * (g - 1))
                    r = rot[:, g % 2].rearrange("p t (a c) -> p t a c", a=2)
                    nc.vector.tensor_tensor(
                        r, qk[:, g % 2].rearrange("p t (a c) -> p t a c", a=2),
                        cos_sb[:, g % 2].unsqueeze(2).to_broadcast([P, TG, 2, C]), ALU.mult).then_inc(cosd, 1)
                    dve.wait_ge(cosd, g + 1)
                    dve.wait_ge(sind, g + 1)
                    rr = rot[:, g % 2].rearrange("p t (a h c) -> p (t a) h c", a=2, h=2)
                    ss = rsin[:].rearrange("p t (a h c) -> p (t a) h c", a=2, h=2)
                    for h in range(2):
                        nc.vector.tensor_tensor(rr[:, :, h, :], rr[:, :, h, :], ss[:, :, 1 - h, :],
                                                ALU.add).then_inc(half_ready, 1)
                elif step[0] == "tqk":
                    g = step[1]
                    for k, (hi, lo, bank) in enumerate(((qh, ql, P0), (kh, kl, P1))):
                        dve.wait_ge(qkhi_ready, 2 * g + k + 1)
                        nc.vector.tensor_tensor(lo[:, W * g:W * g + W], bank[:], hi[:, W * g:W * g + W],
                                                ALU.subtract).then_inc(qklo_ready, 1)
                elif step[0] == "s":
                    i, c = step[1:]
                    cuts = score_chunks(i)
                    if i >= 2 and c == 0:
                        dve.wait_ge(pt_ready, turn_no[i - 2, (i - 2) // TG] + 1)
                        dve.wait_ge(osb_ready, i - 1)
                    elif i < 2 and c == 0:
                        dve.wait_ge(mask_in, 16)
                        dve.wait_ge(ao_ready, G)
                    a, b = cuts[c]
                    n = chunk_no[i, c]
                    dve.wait_ge(s_ready, n + 1)
                    bank = (S0, S1)[n % 2][:, 0:b - a]
                    if c < len(cuts) - 1:
                        nc.vector.tensor_scalar(scores[i % 2][:, a:b], bank, SCALE, MASKED, ALU.mult, ALU.max,
                                                accum_out=cmax[:, i, c:c + 1]).then_inc(sc_ready, 1)
                        continue
                    m0 = MASK_LEAD - (P * i - a)
                    nc.vector.tensor_tensor_reduce(scores[i % 2][:, a:b], bank, mask_sb[:, m0:m0 + b - a], SCALE,
                                                   MASKED, ALU.add, ALU.max, cmax[:, i, c:c + 1]).then_inc(sc_ready, 1)
                    dve.wait_ge(sc_ready, n + 1)
                    nc.vector.tensor_reduce(negm[:, i:i + 1], cmax[:, i, 0:len(cuts)], AX_X, ALU.max,
                                            negate=True).then_inc(m_ready, 1)
                elif step[0] == "o":
                    i = step[1]
                    np_ = len(exp_pieces(i))
                    dve.wait_ge(e_ready, piece_no[i, np_ - 1] + 1)
                    nc.vector.tensor_reduce(psum_all[:, i:i + 1], psums[:, i, 0:np_], AX_X, ALU.add).then_inc(ps_ready, 1)
                    dve.wait_ge(ps_ready, i + 1)
                    nc.vector.reciprocal(rsum[:, i:i + 1], psum_all[:, i:i + 1]).then_inc(rs_ready, 1)
                    dve.wait_ge(pv_ready, turn_no[i, i // TG] + 1)
                    o = O[:, C * (i % TG):C * (i % TG) + C]
                    if i < T - 1:
                        dve.wait_ge(vnext_in[(i + 1) // TG], 16)
                        if i >= 2:
                            dve.wait_ge(x3_ready, i - 1)
                        nc.vector.scalar_tensor_tensor(
                            out=osb[:, i % 2, :], in0=vnext[:, i, :], scalar=scores[i % 2][:, P * (i + 1):P * (i + 1) + 1],
                            in1=o, op0=ALU.mult, op1=ALU.add).then_inc(osb_ready, 1)
                        dve.wait_ge(osb_ready, i + 1)
                        o = osb[:, i % 2, :]
                    dve.wait_ge(rs_ready, i + 1)
                    nc.vector.scalar_tensor_tensor(out=xs[:, i, :], in0=o, scalar=rsum[:, i:i + 1], in1=xs[:, i, :],
                                                   op0=ALU.mult, op1=ALU.add).then_inc(x3_ready, 1)

        @block.tensor
        def _(pe):
            reader = {}

            def claim(bank):
                if bank.name in reader:
                    pe.wait_ge(*reader[bank.name])

            def split_product(dst, stationary, moving):
                (sh, sl), (mh, ml) = stationary, moving
                nc.tensor.matmul(dst, sh, mh, start=True, stop=False)
                nc.tensor.matmul(dst, sh, ml, start=False, stop=False)
                return nc.tensor.matmul(dst, sl, mh, start=False, stop=True)

            for step in plan:
                if step[0] == "turn":
                    n, g = step[1:]
                    lane, j = lane_job(n, g)
                    bank = (MB, H1)[j % 2] if n == 0 else MB
                    if n == 0 and g == 0:
                        pe.wait_ge(id_in, 16)
                    pe.wait_ge(xn_ready[n], g + 1)
                    claim(bank)
                    for t in range(TG):
                        last = nc.tensor.transpose(bank[:, C * t:C * t + C], xn[lane][:, j % 2, t, :], id_sb[:])
                    last.then_inc(xT_ready[lane], 1)
                    reader[bank.name] = (lo_ready[lane], j + 1)
                elif step[0] == "q":
                    g = step[1]
                    pe.wait_ge(lo_ready[0], g + 1)
                    pe.wait_ge(w_lo, 1)
                    claim(O)
                    split_product(O[:], (wh[:, 0:C], wl[:, 0:C]),
                                  (xh[0][:, g % 2, :], xl[0][:, g % 2, :])).then_inc(q_ready, 1)
                    reader[O.name] = (rq_ready, g + 1)
                elif step[0] == "kv":
                    g = step[1]
                    pe.wait_ge(lo_ready[0], g + 1)
                    pe.wait_ge(w_lo, 1)
                    for pr in range(2):
                        bank = ((S0, S1), (P0, P1))[g % 2][pr]
                        claim(bank)
                        for t in range(2):
                            o = C * (2 * pr + t)
                            last = split_product(
                                bank[:, 2 * C * t:2 * C * t + 2 * C],
                                (xh[0][:, g % 2, o:o + C], xl[0][:, g % 2, o:o + C]), (wh[:, C:3 * C], wl[:, C:3 * C]))
                        last.then_inc(kv_ready, 1)
                        reader[bank.name] = (vone_ready, 2 * g + pr + 1)
                elif step[0] == "acc":
                    g = step[1]
                    if g == 0:
                        pe.wait_ge(vone_set, 1)
                    pe.wait_ge(kphi_ready, 2 * g + 2)
                    pe.wait_ge(vone_ready, 2 * g + 2)
                    for t in range(TG * g, TG * g + TG):
                        last = nc.tensor.matmul(H0[:, 0:C + 1], kphi[:, C * t:C * t + C], vone[:, t, :],
                                                start=(t == 0), stop=(t == T - 1))
                    if g == G - 1:
                        last.then_inc(sum_ready, 1)
                        reader[H0.name] = (diag_ready, 2)
                elif step[0] == "ao":
                    g = step[1]
                    pe.wait_ge(diag_ready, 2)
                    pe.wait_ge(qphi_ready, g + 1)
                    claim(P0)
                    claim(P1)
                    for t in range(TG):
                        q_t = qphi[:, W * g + P * t:W * g + P * t + P]
                        nc.tensor.matmul(P0[:, C * t:C * t + C], q_t, bdkv[:], start=True, stop=True)
                        last = nc.tensor.matmul(P1[:, HEADS * t:HEADS * t + HEADS], q_t, bdks[:], start=True, stop=True)
                    last.then_inc(ao_ready, 1)
                    reader[P0.name] = reader[P1.name] = (heads_ready, g + 1)
                elif step[0] == "at":
                    g = step[1]
                    pe.wait_ge(heads_ready, g + 1)
                    claim(O)
                    for t in range(TG):
                        last = nc.tensor.transpose(O[:, C * t:C * t + C], ebuf[:, g % 2, C * t:C * t + C], id_sb[:])
                    last.then_inc(aT_ready, 1)
                    reader[O.name] = (aTs_ready, g + 1)
                elif step[0] == "pr":
                    g = step[1]
                    pe.wait_ge(aTs_ready, g + 1)
                    claim(P1)
                    for t in range(TG):
                        last = nc.tensor.matmul(P1[:, C * t:C * t + C], rbuf[:, g % 2, C * t:C * t + C], wp[:],
                                                start=True, stop=True)
                    last.then_inc(pr_ready, 1)
                    reader[P1.name] = (x1_ready, g + 1)
                elif step[0] == "f1":
                    j, m = step[1:]
                    pe.wait_ge(w_lo, 2)
                    pe.wait_ge(lo_ready[1], j + 1)
                    bank = (H0, H1)[m % 2]
                    o = f_of + P * m
                    claim(bank)
                    split_product(bank[:], (wh[:, o:o + P], wl[:, o:o + P]),
                                  (xh[1][:, j % 2, :], xl[1][:, j % 2, :])).then_inc(h_ready, 1)
                    reader[bank.name] = (relu_ready, M * j + m + 1)
                elif step[0] == "f2":
                    j, t = step[1:]
                    if t == 0:
                        if j == 0:
                            pe.wait_ge(wd_in, 16)
                        for n in range(M * j, M * j + M):
                            pe.wait_ge(*squared(n))
                        claim(MB)
                    for m in range(M):
                        last = nc.tensor.matmul(MB[:, C * t:C * t + C], hid[:, j % 2, m, P * t:P * t + P],
                                                wd[:, m, :], start=(m == 0), stop=(m == M - 1))
                    if t == TG - 1:
                        last.then_inc(y_ready, 1)
                        reader[MB.name] = (ysb_ready, j + 1)
                elif step[0] == "count":
                    j = step[1]
                    pe.wait_ge(consts, 1)
                    claim(H0)
                    nc.tensor.matmul(H0[:], fives[:], ones[:], start=True, stop=False)
                    for k in range(STEPS):
                        pe.wait_ge(sign_ready, STEPS * j + k + 1)
                        last = nc.tensor.matmul(H0[:], half_id[:], sign[:, k, :], start=False, stop=(k == STEPS - 1))
                    last.then_inc(count_ready, 1)
                    reader[H0.name] = (xf_ready, j + 1)
                elif step[0] == "qkv":
                    g = step[1]
                    pe.wait_ge(w_lo, 3)
                    pe.wait_ge(lo_ready[0], G + g + 1)
                    for t in range(TG):
                        n = TG * g + t
                        bank = (S0, S1)[n % 2]
                        claim(bank)
                        split_product(bank[:, 0:3 * C], (xh[0][:, g % 2, P * t:P * t + P], xl[0][:, g % 2, P * t:P * t + P]),
                                      (wh[:, r_of:r_of + WR], wl[:, r_of:r_of + WR])).then_inc(qkv_ready, 1)
                        reader[bank.name] = (v_ready, n + 1)
                elif step[0] == "tqk":
                    g = step[1]
                    pe.wait_ge(half_ready, 2 * g + 2)
                    for k, bank in enumerate((P0, P1)):
                        claim(bank)
                        for t in range(TG):
                            last = nc.tensor.transpose(bank[:, P * t:P * t + P], rot[:, g % 2, t, C * k:C * k + C], id_sb[:])
                        last.then_inc(tqk_ready, 1)
                        reader[bank.name] = (qklo_ready, 2 * g + k + 1)
                elif step[0] == "s":
                    i, c = step[1:]
                    a, b = score_chunks(i)[c]
                    n = chunk_no[i, c]
                    bank = (S0, S1)[n % 2]
                    if c == 0:
                        pe.wait_ge(qklo_ready, 2 * (min(i + 1, T - 1) // TG) + 2)
                    claim(bank)
                    split_product(bank[:, 0:b - a], (qh[:, P * i:P * i + P], ql[:, P * i:P * i + P]),
                                  (kh[:, a:b], kl[:, a:b])).then_inc(s_ready, 1)
                    reader[bank.name] = (sc_ready, n + 1)
                elif step[0] == "t":
                    i, jg = step[1:]
                    n = turn_no[i, jg]
                    nb = min(TG, i + 1 - TG * jg)
                    end = P * (TG * jg + nb)
                    piece = next(p for p, (a, b) in enumerate(exp_pieces(i)) if end <= b)
                    bank = (P0, P1)[n % 2]
                    pe.wait_ge(e_ready, piece_no[i, piece] + 1)
                    claim(bank)
                    for b in range(nb):
                        k0 = P * (TG * jg + b)
                        last = nc.tensor.transpose(bank[:, P * b:P * b + P], scores[i % 2][:, k0:k0 + P], id_sb[:])
                    last.then_inc(pt_ready, 1)
                    reader[bank.name] = (ptc_ready, n + 1)
                elif step[0] == "pv":
                    i, jg = step[1:]
                    n = turn_no[i, jg]
                    nb = min(TG, i + 1 - TG * jg)
                    pe.wait_ge(ptc_ready, n + 1)
                    if jg == 0:
                        claim(O)
                    for b in range(nb):
                        k = TG * jg + b
                        last = nc.tensor.matmul(O[:, C * (i % TG):C * (i % TG) + C], pt[:, n % 3, P * b:P * b + P],
                                                v[:, k, :], start=(k == 0), stop=(k == i))
                    last.then_inc(pv_ready, 1)
                    if k == i:
                        reader[O.name] = (x3_ready, i + 1)


def rotary_tables():
    i = np.arange(HALF, dtype=np.float32)
    theta = np.power(np.float32(10000.0), np.float32(-2.0) * i / np.float32(C)).astype(np.float32)
    ang = np.arange(N_TOK, dtype=np.float32)[:, None] * theta[None, :]
    c, s = np.cos(ang), np.sin(ang)
    return np.concatenate([c, c], 1), np.concatenate([s, -s], 1)


def score_mask():
    q, k = np.arange(P)[:, None], np.arange(MASK_W)[None, :] - MASK_LEAD
    return np.where(k <= q + EXTRA, 0.0, MASKED).astype(np.float32)


def head_masks():
    own = (np.arange(C)[:, None] // HD == np.arange(C)[None, :] // HD)
    per = (np.arange(C)[:, None] // HD == np.arange(HEADS)[None, :])
    return np.concatenate([own, per], 1).astype(np.float32)


def kernel(L0_attn_a_x, L0_attn_a_Wqkv, L0_attn_a_Wproj, L0_attn_a_bproj, L0_attn_b_Wq, L0_attn_b_Wk,
           L0_attn_b_Wv, L0_ffn_W_fc, L0_ffn_W_proj):
    import concourse.bacc as _bacc
    from concourse.bass_utils import run_bass_kernel_spmd as _run

    lay = np.ascontiguousarray
    order = np.concatenate([np.arange(0, C, 2), np.arange(1, C, 2)])
    rope_rows = np.concatenate([np.asarray(L0_attn_b_Wq)[order], np.asarray(L0_attn_b_Wk)[order],
                                np.asarray(L0_attn_b_Wv)])
    cos, sin = rotary_tables()
    arrays = {
        "x": lay(np.asarray(L0_attn_a_x).reshape(N_TOK, C)),
        "w_qkv": lay(np.asarray(L0_attn_a_Wqkv).T),
        "w_proj": lay(np.asarray(L0_attn_a_Wproj).T),
        "b_proj": lay(np.asarray(L0_attn_a_bproj)),
        "w_fc": lay(np.asarray(L0_ffn_W_fc).T),
        "w_down": lay(np.asarray(L0_ffn_W_proj).T.reshape(M, P, C).transpose(1, 0, 2).reshape(P, M * C)),
        "w_rope": lay(rope_rows.T),
        "cos": lay(cos.astype(np.float32)),
        "sin": lay(sin.astype(np.float32)),
        "ident": np.eye(P, dtype=np.float32),
        "mask": score_mask(),
        "heads": head_masks(),
    }
    nc = _bacc.Bacc("TRN2", target_bir_lowering=False, num_devices=1)
    args = [nc.dram_tensor(f"in_{n}", a.shape, mybir.dt.from_np(a.dtype), kind="ExternalInput").ap()
            for n, a in arrays.items()]
    args.append(nc.dram_tensor("out_x", (N_TOK, C), F32, kind="ExternalOutput").ap())
    hybrid_block(nc, *args)
    r = _run(nc, [{f"in_{n}": a for n, a in arrays.items()}], core_ids=[0])
    return r.results[0]["out_x"].reshape(1, N_TOK, C)
```

```python
from contextlib import ExitStack

import numpy as np

import concourse.bass as bass
from concourse import mybir

F32 = mybir.dt.float32
F32R = mybir.dt.float32r
BF16 = mybir.dt.bfloat16
ALU = mybir.AluOpType
ACT = mybir.ActivationFunctionType
AX_X = mybir.AxisListType.X

P = 128
C = 128
N_TOK = 2048
T = N_TOK // P
TG = 4
G = T // TG
W = TG * P
HEADS = 16
HD = C // HEADS
F = 512
M = F // P
HALF = C // 2
EPS_LN = 1e-5
EPS_ATT = 1e-6
SCALE = float(1.0 / np.sqrt(np.float32(C)))
BETA, THRESHOLD, STEPS = 0.9, 1.0, 5
MASKED = -3.0e38
EXTRA = 1
MASK_LEAD = W - P
MASK_W = MASK_LEAD + 2 * P
EXP_PIECE = 1024
GROUPS = [(TG * g, TG) for g in range(G)]
MLP_JOBS = [[(0, 2), (2, 2)] + GROUPS[1:], GROUPS[:-1] + [(12, 2), (14, 1), (15, 1)]]
NORM_JOBS = [GROUPS, MLP_JOBS[0], GROUPS, MLP_JOBS[1]]
JOBS = MLP_JOBS[0] + MLP_JOBS[1]
J1 = len(MLP_JOBS[0])
WARM_UP = 16
MEMS = 2 * (STEPS - 1) - 1
JUST_BELOW_1 = 1.0 - 2.0 ** -24


def score_chunks(i):
    width = N_TOK if i == T - 1 else max(256, P * (i + 1) + 2 * EXTRA)
    cuts, at = [], 0
    while width - at > W:
        step = W if width - at - W >= 256 else width - at - 256
        cuts.append((at, at + step))
        at += step
    cuts.append((at, width))
    return cuts


def exp_pieces(i):
    width = score_chunks(i)[-1][1]
    return [(a, min(a + EXP_PIECE, width)) if width - a - EXP_PIECE > 256 else (a, width)
            for a in range(0, width, EXP_PIECE) if a == 0 or width - (a - EXP_PIECE) - EXP_PIECE > 256]


PLAN = {
    "pe": """
turn-0-0 turn-0-1 q-0 kv-0-0 kv-0-1 kv-1-0 q-1 turn-0-2 kv-1-1 turn-0-3 acc-0 kv-2-0 kv-2-1 kv-3-0 acc-1 kv-3-1
q-2 acc-2 acc-3 q-3 ao-0 ao-1 at-0 pr-0 at-1 ao-2 pr-1 turn-1-0 at-2 f1-0-0 f1-0-1 turn-1-1 f1-0-2 f1-0-3 pr-2
f1-1-0 f2-0-0 f2-0-1 f1-1-1 f1-1-2 turn-1-2 f1-1-3 ao-3 turn-1-3 f1-2-0 f1-2-1 f2-1-0 f2-1-1 f1-2-2 f1-2-3
f1-3-0 at-3 f1-3-1 count-0 pr-3 count-1 f2-2-0 f2-2-1 f2-2-2 f2-2-3 turn-2-0 f1-3-2 f1-3-3 turn-1-4 qkv-0-0
qkv-0-1 qkv-0-2 qkv-0-3 f1-4-0 f2-3-0 f2-3-1 count-2 f1-4-1 tqk-0-0 tqk-0-1 f2-3-2 f2-3-3 f1-4-2 s-0-0 s-1-0
turn-2-1 f1-4-3 qkv-1-0 pt-0-0 qkv-1-1 qkv-1-2 pv-0-0 qkv-1-3 f2-4-0 f2-4-1 s-2-0 pt-1-0 count-3 f2-4-2 tqk-1-0
tqk-1-1 f2-4-3 pv-1-0 pt-2-0 s-3-0 s-3-1 pv-2-0 s-4-0 s-4-1 turn-2-2 pt-3-0 s-5-0 pv-3-0 qkv-2-0 qkv-2-1 pt-4-0
qkv-2-2 qkv-2-3 s-5-1 pt-4-1 s-6-0 pv-4-0 pv-4-1 s-6-1 turn-3-0 pt-5-0 pt-5-1 count-4 tqk-2-0 tqk-2-1 pv-5-0
pv-5-1 f1-5-0 f1-5-1 pt-6-0 s-7-0 pt-6-1 s-7-1 f1-5-2 s-7-2 pv-6-0 pv-6-1 s-8-0 turn-2-3 pt-7-0 s-8-1 pt-7-1
s-8-2 pv-7-0 pv-7-1 s-9-0 qkv-3-0 pt-8-0 f1-5-3 s-9-1 pt-8-1 s-9-2 pv-8-0 qkv-3-1 pt-8-2 qkv-3-2 pv-8-1 qkv-3-3
pv-8-2 turn-3-1 pt-9-0 pt-9-1 s-10-0 pv-9-0 pt-9-2 s-10-1 pv-9-1 s-10-2 pv-9-2 tqk-3-0 f1-6-0 tqk-3-1 f2-5-0
f1-6-1 f2-5-1 s-11-0 pt-10-0 pt-10-1 s-11-1 f2-5-2 s-11-2 s-11-3 f1-6-2 pt-10-2 pv-10-0 pv-10-1 pt-11-0 pv-10-2
s-12-0 s-12-1 pt-11-1 pv-11-0 pt-11-2 s-12-2 s-12-3 pv-11-1 pv-11-2 s-13-0 f1-6-3 f2-5-3 s-13-1 pt-12-0 s-13-2
s-13-3 pt-12-1 pt-12-2 pv-12-0 turn-3-2 pt-12-3 pv-12-1 pv-12-2 pv-12-3 f1-7-0 s-14-0 pt-13-0 pt-13-1 f1-7-1
f1-7-2 f2-6-0 pv-13-0 s-14-1 pt-13-2 s-14-2 pv-13-1 s-14-3 pt-13-3 s-15-0 pv-13-2 f2-6-1 pv-13-3 f1-7-3 f2-6-2
pt-14-0 s-15-1 f2-6-3 pt-14-1 s-15-2 s-15-3 count-5 pt-14-2 turn-3-3 pv-14-0 pv-14-1 pt-14-3 f1-8-0 f2-7-0
f1-8-1 f2-7-1 f1-8-2 f2-7-2 pv-14-2 f2-7-3 pv-14-3 pt-15-0 pt-15-1 f1-8-3 count-6 pt-15-2 pt-15-3 pv-15-0
pv-15-1 turn-3-4 pv-15-2 pv-15-3 f1-9-0 f1-9-1 f2-8-0 f1-9-2 f2-8-1 f1-9-3 count-7 turn-3-5 f2-9-0 f1-10-0
f1-10-1 f1-10-2 f1-10-3 count-8 f2-10-0 count-9 count-10
""",
    "act": """
w_hi-0 hi-0-0 hi-0-1 q_exp-0 kv_exp-0-0 kv_exp-0-1 kv_exp-1-0 hi-0-2 kv_exp-1-1 hi-0-3 q_exp-1 kv_exp-2-0
kv_exp-2-1 kv_exp-3-0 kv_exp-3-1 q_exp-2 w_hi-1 q_exp-3 w_hi-2 aT_copy-0 aT_copy-1 norm-1-0 hi-1-0 aT_copy-2
relu-0-0 relu-0-1 hi-1-1 sq-0-0 relu-0-2 relu-0-3 sq-0-3 relu-1-0 y-0 u_first-0 relu-1-1 sign-0-0 sq-1-0 hi-1-2
relu-1-2 relu-1-3 sign-0-1 hi-1-3 full-1-3 sign-0-2 sign-0-3 relu-2-0 sign-0-4 relu-2-1 y-1 u_first-1 relu-2-2
sign-1-0 relu-2-3 sign-1-1 sign-1-2 relu-3-0 aT_copy-3 sign-1-3 sign-1-4 relu-3-1 y-2 u_first-2 sign-2-0 hi-2-0
relu-3-2 sign-2-1 relu-3-3 hi-1-4 qkv_copy-0-0 qkv_copy-0-1 sign-2-2 qkv_copy-0-2 qkv_copy-0-3 relu-4-0 sign-2-3
sign-2-4 qk_hi-0-0 sq-4-0 qk_hi-0-1 relu-4-1 y-3 u_first-3 sign-3-0 relu-4-2 hi-2-1 e-0-0 sign-3-1 relu-4-3
qkv_copy-1-0 pt_copy-0-0 qkv_copy-1-1 sign-3-2 qkv_copy-1-2 qkv_copy-1-3 sign-3-3 e-1-0 sign-3-4 e-2-0
pt_copy-1-0 qk_hi-1-0 qk_hi-1-1 y-4 u_first-4 pt_copy-2-0 norm-2-2 e-3-0 hi-2-2 pt_copy-3-0 full-2-2 sign-4-0
e-4-0 sign-4-1 sign-4-2 qkv_copy-2-0 qkv_copy-2-1 qkv_copy-2-2 qkv_copy-2-3 sign-4-3 norm-3-0 e-5-0 sign-4-4
hi-3-0 pt_copy-5-0 full-3-0 pt_copy-5-1 qk_hi-2-0 qk_hi-2-1 e-6-0 relu-5-0 relu-5-1 sq-5-0 pt_copy-6-0 e-7-0
hi-2-3 pt_copy-7-1 e-8-0 sq-5-1 qkv_copy-3-0 relu-5-2 pt_copy-8-0 relu-5-3 e-9-0 qkv_copy-3-1 qkv_copy-3-2 e-9-1
qkv_copy-3-3 pt_copy-9-0 pt_copy-9-1 hi-3-1 qk_hi-3-0 relu-6-0 qk_hi-3-1 e-10-0 relu-6-1 e-10-1 pt_copy-10-1
e-11-0 e-11-1 relu-6-2 pt_copy-11-1 sq-6-1 e-12-0 sq-6-2 y-5 sign-5-0 e-12-1 u_first-5 pt_copy-12-1 pt_copy-12-2
hi-3-2 pt_copy-12-3 e-13-0 relu-6-3 relu-7-0 sign-5-1 e-13-1 relu-7-1 sq-7-0 sign-5-2 sign-5-3 e-14-0 e-14-1
pt_copy-14-0 sign-5-4 relu-7-2 y-6 pt_copy-14-1 sq-7-2 u_first-6 relu-7-3 e-15-0 hi-3-3 e-15-1 pt_copy-14-2
relu-8-0 sign-6-0 sign-6-1 relu-8-1 sq-8-0 sign-6-2 sq-8-1 sign-6-3 relu-8-2 sign-6-4 y-7 u_first-7 pt_copy-15-0
pt_copy-15-1 pt_copy-15-2 relu-8-3 sign-7-0 sign-7-1 pt_copy-15-3 sign-7-2 hi-3-4 relu-9-0 relu-9-1 sign-7-3
sq-9-0 relu-9-2 sign-7-4 y-8 u_first-8 sq-9-1 relu-9-3 sq-9-2 sq-9-3 hi-3-5 sign-8-0 sign-8-1 sign-8-2 y-9
relu-10-0 sign-8-3 u_first-9 relu-10-1 relu-10-2 sign-8-4 sign-9-0 relu-10-3 sq-10-3 sign-9-1 sign-9-2 sign-9-3
y-10 u_first-10 sign-9-4 sign-10-0 sign-10-1 sign-10-2 sign-10-3 sign-10-4
""",
    "dve": """
stats-0-0 stats-0-1 norm-0-0 stats-0-2 norm-0-1 lo-0-0 stats-0-3 lo-0-1 norm-0-2 k_phi-0-0 norm-0-3 k_phi-0-1
lo-0-2 k_phi-1-0 k_phi-1-1 lo-0-3 q_phi-0 k_phi-2-0 k_phi-2-1 q_phi-1 k_phi-3-0 k_phi-3-1 q_phi-2 diag w_lo-1
q_phi-3 heads-0 heads-1 x1-0 stats-1-0 stats-1-1 heads-2 x1-1 lo-1-0 norm-1-1 stats-1-2 sq-0-1 lo-1-1 sq-0-2
x1-2 stats-1-3 norm-1-2 mem-0-0 norm-1-3 lo-1-2 sq-1-2 mem-0-1 mem-0-2 mem-0-3 heads-3 sq-2-1 mem-1-0 mem-1-1
mem-1-2 mem-1-3 xf-0 xf-1 stats-2-0 x1-3 stats-1-4 norm-2-0 mem-2-0 norm-1-4 lo-2-0 mem-2-1 lo-1-4 mem-2-2
mem-2-3 cos-0 rot-0-0 xf-2 stats-2-1 qk_lo-0-0 qk_lo-0-1 norm-2-1 score_copy-0-0 score_copy-1-0 mem-3-0 lo-2-1
mem-3-1 row_sum-0 mem-3-2 o-0 mem-3-3 cos-1 score_copy-2-0 rot-1-1 xf-3 stats-2-2 qk_lo-1-0 qk_lo-1-1 row_sum-1
o-1 row_sum-2 score_copy-3-0 score_copy-3-1 o-2 mem-4-0 score_copy-4-0 score_copy-4-1 mem-4-1 row_sum-3 o-3
score_copy-5-0 stats-3-0 mem-4-2 pt_copy-4-0 score_copy-5-1 pt_copy-4-1 mem-4-3 cos-2 row_sum-4 o-4 rot-2-0
score_copy-6-0 score_copy-6-1 row_sum-5 xf-4 qk_lo-2-0 o-5 qk_lo-2-1 stats-2-3 score_copy-7-0 row_sum-6
pt_copy-6-1 score_copy-7-1 score_copy-7-2 norm-2-3 o-6 score_copy-8-0 pt_copy-7-0 score_copy-8-1 lo-2-3
score_copy-8-2 row_sum-7 o-7 stats-3-1 score_copy-9-0 score_copy-9-1 score_copy-9-2 pt_copy-8-1 pt_copy-8-2
norm-3-1 row_sum-8 o-8 row_sum-9 cos-3 score_copy-10-0 lo-3-1 rot-3-0 pt_copy-9-2 rot-3-1 o-9 score_copy-10-1
score_copy-10-2 qk_lo-3-0 qk_lo-3-1 pt_copy-10-0 score_copy-11-0 score_copy-11-1 score_copy-11-2 score_copy-11-3
row_sum-10 pt_copy-10-2 row_sum-11 pt_copy-11-0 o-10 score_copy-12-0 score_copy-12-1 pt_copy-11-2
score_copy-12-2 score_copy-12-3 o-11 score_copy-13-0 stats-3-2 score_copy-13-1 pt_copy-12-0 norm-3-2
score_copy-13-2 score_copy-13-3 row_sum-12 lo-3-2 mem-5-0 sq-6-3 o-12 score_copy-14-0 pt_copy-13-0 pt_copy-13-1
mem-5-1 mem-5-2 score_copy-14-1 score_copy-14-2 pt_copy-13-2 row_sum-13 mem-5-3 pt_copy-13-3 score_copy-14-3
o-13 stats-3-3 sq-7-1 score_copy-15-0 score_copy-15-1 norm-3-3 score_copy-15-2 score_copy-15-3 mem-6-0 xf-5
lo-3-3 row_sum-14 mem-6-1 mem-6-2 pt_copy-14-3 mem-6-3 row_sum-15 o-14 stats-3-4 mem-7-0 mem-7-1 norm-3-4 xf-6
mem-7-2 mem-7-3 o-15 stats-3-5 norm-3-5 mem-8-0 mem-8-1 xf-7 mem-8-2 mem-8-3 mem-9-0 sq-10-2 mem-9-1 mem-9-2
xf-8 mem-9-3 mem-10-0 mem-10-1 mem-10-2 mem-10-3 xf-9 xf-10
""",
    "pool": """
rstd-0-0 half_id rstd-0-1 w_lo-0 rstd-0-2 bias-0 rstd-0-3 bias-1 bias-2 vnext_zero w_lo-2 rstd-1-0 nmr-1-0
rstd-1-1 rstd-1-2 bias-3 rstd-1-3 sq-1-1 sq-1-3 lo-1-3 sq-2-0 sq-2-2 sq-2-3 sq-3-0 rstd-2-0 rstd-1-4 sq-3-1
sq-3-2 sq-3-3 sin-0 rot-0-1 rstd-2-1 sq-4-1 sq-4-2 sq-4-3 sin-1 rot-1-0 rstd-2-2 nmr-2-2 lo-2-2 rstd-3-0 nmr-3-0
sin-2 rot-2-1 lo-3-0 rstd-2-3 sq-5-2 rstd-3-1 sin-3 sq-5-3 sq-6-0 rstd-3-2 rstd-3-3 sq-7-3 sq-8-2 rstd-3-4
sq-8-3 rstd-3-5 sq-10-0 sq-10-1
""",
}


def make_plan():
    return {engine: [(name, *map(int, rest)) for name, *rest in (word.split("-") for word in steps.split())]
            for engine, steps in PLAN.items()}


def hybrid_block(nc, x, w_qkv, w_proj, b_proj, w_fc, w_down, w_rope, cos, sin, ident, mask, heads, out):
    plan = make_plan()
    chunk_no = {at: n for n, at in enumerate((i, c) for i in range(T) for c in range(len(score_chunks(i))))}
    piece_no = {at: n for n, at in enumerate((i, p) for i in range(T) for p in range(len(exp_pieces(i))))}
    turn_no = {at: n for n, at in enumerate((i, jg) for i in range(T) for jg in range(i // TG + 1))}

    with ExitStack() as ctx:
        def sb(name, *shape, dt=F32):
            return ctx.enter_context(nc.sbuf_tensor(name, [P, *shape], dt))

        def sem(name):
            return ctx.enter_context(nc.semaphore(name))

        def sems(name, n):
            return [sem(f"{name}{i}") for i in range(n)]

        S0, S1, P0, P1, O, H0, H1, MB = (
            ctx.enter_context(nc.psum_tensor(f"bank_{n}", [P, W], F32))
            for n in ("s0", "s1", "p0", "p1", "o", "h0", "h1", "m"))

        xs = sb("xs", T, C)
        stat = sb("stat", 4, T, 6)
        mom = sb("mom", 4, T, 2)
        veps = sb("veps", 4, T)
        rstd = sb("rstd", 4, T)
        nmean = sb("nmean", 4, T)
        nmr = sb("nmr", 4, T)
        mhalf = sb("mhalf", TG)
        xn = [sb(f"xn{k}", 2, TG, C) for k in range(2)]
        xh = [sb(f"xh{k}", 2, W, dt=F32R) for k in range(2)]
        xl = [sb(f"xl{k}", 2, W, dt=F32R) for k in range(2)]
        ebuf = sb("ebuf", 2, W)
        rbuf = sb("rbuf", 2, W)
        qphi = sb("qphi", N_TOK)
        kphi = sb("kphi", N_TOK)
        vone = sb("vone", T, C + 1)
        bdkv = sb("bdkv", C)
        bdks = sb("bdks", HEADS)
        den = sb("den", TG * HEADS)
        rec = sb("rec", TG * HEADS)
        relu = sb("relu", 2, W)
        ek, rk = (relu[:, k, :].rearrange("p (r t c) -> p r t c", r=2, t=2) for k in range(2))
        hid = sb("hid", 2, M, W)
        y = sb("y", 2, W)
        u = sb("u", W)
        u_first = sb("u_first", 2, W)
        mem = sb("mem", 2, W)
        sign = sb("sign", STEPS, W, dt=BF16)
        half_id = sb("half_id", P, dt=BF16)
        fives = sb("fives", P, dt=BF16)
        ones = sb("ones", W, dt=BF16)
        above = sb("above", 1)
        qk = sb("qk", 2, TG, 2 * C)
        rot = sb("rot", 2, TG, 2 * C)
        rsin = sb("rsin", TG, 2 * C)
        cos_sb = sb("cos_sb", 2, TG, C)
        sin_sb = sb("sin_sb", 2, TG, C)
        qh, ql, kh, kl = (sb(n, N_TOK, dt=F32R) for n in ("qh", "ql", "kh", "kl"))
        v = vone[:, :, 0:C]
        vnext = sb("vnext", T, C)
        cmax = sb("cmax", T, 4)
        negm = sb("negm", T)
        psums = sb("psums", T, 2)
        psum_all = sb("psum_all", T)
        rsum = sb("rsum", T)
        pt = sb("pt", 3, W)
        osb = sb("osb", 2, C)
        WA, WF, WR = 3 * C, F, 3 * C
        wh = sb("wh", WA + WF + WR, dt=F32R)
        wl = sb("wl", WA + WF + WR, dt=F32R)
        w_fc_sb = sb("w_fc_sb", WF)
        xfull = sb("xfull", 2, W)
        x_one = sb("x_one", 2, P)
        wp = sb("wp", C)
        wd = sb("wd", M, C)
        bias = sb("bias", C)
        id_sb = sb("id_sb", P)
        mask_sb = sb("mask_sb", MASK_W)
        heads_sb = sb("heads_sb", C + HEADS)
        a_of, f_of, r_of = 0, WA, WA + WF
        WEIGHTS = ((a_of, WA), (f_of, WF), (r_of, WR))
        qkfull = ebuf
        raw = hid[:].rearrange("p a m w -> p (a m w)")
        RAW = (raw[:, 0:WA], w_fc_sb[:], raw[:, WA:WA + WR])
        scores = [qphi, kphi]

        x_in = sems("x_in", G)
        wa_in, wf_in, wr_in, id_in, small_in, wd_in, mask_in = (
            sem(n) for n in ("wa_in", "wf_in", "wr_in", "id_in", "small_in", "wd_in", "mask_in"))
        trig_in = sems("trig_in", G)
        vnext_in, stored = sems("vnext_in", G), sem("stored")
        warm, half_ready_id = sem("warm"), sem("half_id_ready")
        w_hi, w_lo, consts = sem("w_hi"), sems("w_lo", 3), sem("consts")
        vnext_zero, vone_set = sem("vnext_zero"), sem("vone_set")
        bn_done, mom_ready, veps_ready, nmean_ready, rstd_ready, nmr_ready = (
            sems(n, 4) for n in ("bn_done", "mom_ready", "veps_ready", "nmean_ready", "rstd_ready", "nmr_ready"))
        xT_ready, hi_ready, lo_ready = (sems(n, 2) for n in ("xT_ready", "hi_ready", "lo_ready"))
        xfull_ready = sems("xfull_ready", 2)
        half_ready = sems("half_ready", 2)
        (q_ready, eq_ready, rq_ready, qphi_ready, kv_ready, ek_ready, rk_ready, vone_ready, kphi_ready, sum_ready,
         diag_ready, ao_ready, den_ready, rec_ready, heads_ready, aT_ready, aTs_ready, pr_ready, xb_ready,
         x1_ready) = (sem(n) for n in (
             "q_ready", "eq_ready", "rq_ready", "qphi_ready", "kv_ready", "ek_ready", "rk_ready", "vone_ready",
             "kphi_ready", "sum_ready", "diag_ready", "ao_ready", "den_ready", "rec_ready", "heads_ready",
             "aT_ready", "aTs_ready", "pr_ready", "xb_ready", "x1_ready"))
        h_ready, relu_ready, y_ready, ysb_ready, u_first_ready, mem_ready, sign_ready, count_ready, xf_ready = (
            sem(n) for n in ("h_ready", "relu_ready", "y_ready", "ysb_ready", "u_first_ready", "mem_ready",
                             "sign_ready", "count_ready", "xf_ready"))
        (qkv_ready, v_ready, cosd, sind, qkfull_ready, tqk_ready, qkhi_ready, qklo_ready, s_ready, sc_ready,
         m_ready, e_ready, pt_ready, pv_ready, ps_ready, rs_ready, osb_ready, x3_ready) = (
             sem(n) for n in (
                 "qkv_ready", "v_ready", "cosd", "sind", "qkfull_ready", "tqk_ready", "qkhi_ready", "qklo_ready",
                 "s_ready", "sc_ready", "m_ready", "e_ready", "pt_ready", "pv_ready",
                 "ps_ready", "rs_ready", "osb_ready", "x3_ready"))

        shared = {"norm": "xn_ready", "sq": "squared", "pt_copy": "pt_copied"}
        done, engine_of = {}, {}
        for engine, steps in plan.items():
            for kind, signal in shared.items():
                mine = [step[1:] for step in steps if step[0] == kind]
                if mine:
                    ready = sem(f"{signal}_{engine}")
                    for n, number in enumerate(mine):
                        done[kind, *number] = ready, n + 1
                        engine_of[kind, *number] = engine

        pooled = [step for step in plan["pool"] if step[0] in ("lo", "qk_lo")]

        def full_number(step):
            mine = [s[1:] for s in pooled if s[0] == step[0] and (s[0] == "qk_lo" or s[1] % 2 == step[1] % 2)]
            return mine.index(step[1:]) + 1

        def bank_freed(step, low_ready, copied):
            return (copied, full_number(step)) if step in pooled else low_ready

        def narrow(j):
            return 2 * P * JOBS[j][1] <= W

        def sign_columns(j):
            first = (j % 2) * W // 2 if narrow(j) else 0
            return slice(first, first + P * JOBS[j][1])

        def sign_user(j):
            return j - 2 if j >= 2 and narrow(j) and narrow(j - 1) else None if j == 1 and narrow(0) else j - 1

        def one(signal):
            return signal[0], 1

        def on_act_before(norm, g):
            return sum(engine_of["norm", norm, k] == "act" for k in range(g))

        def raw_used(eng):
            eng.wait_ge(w_lo[0], 1)
            eng.wait_ge(w_lo[2], 1)

        def rotate(eng, g, h):
            eng.wait_ge(cosd, g + 1)
            eng.wait_ge(sind, g + 1)
            rr = rot[:, g % 2].rearrange("p t (a h c) -> p (t a) h c", a=2, h=2)
            ss = rsin[:].rearrange("p t (a h c) -> p (t a) h c", a=2, h=2)
            eng.tensor_tensor(rr[:, :, h, :], rr[:, :, h, :], ss[:, :, 1 - h, :], ALU.add).then_inc(half_ready[h], 1)

        def lane_job(norm, g):
            return norm % 2, (norm // 2) * (J1 if norm % 2 else G) + g

        def lane_used(eng, lane, j):
            if j < 2:
                return
            if lane == 1:
                eng.wait_ge(h_ready, M * (j - 1))
            elif j - 2 < G:
                eng.wait_ge(q_ready, j - 1)
                eng.wait_ge(kv_ready, 2 * (j - 1))
            else:
                eng.wait_ge(qkv_ready, TG * (j - 1 - G))

        block = ctx.enter_context(nc.Block())

        @block.sync
        def _(sp):
            x_t = x.rearrange("(t p) c -> p t c", p=P)
            o_t = out.rearrange("(t p) c -> p t c", p=P)
            for g in range(G):
                sp.dma_start(xs[:, TG * g:TG * g + TG, :], x_t[:, TG * g:TG * g + TG, :]).then_inc(x_in[g], 16)
            for dst, src, arrived in ((RAW[1], w_fc, wf_in),
                                      (wd[:].rearrange("p m c -> p (m c)"), w_down, wd_in),
                                      (RAW[2], w_rope, wr_in), (mask_sb[:], mask, mask_in)):
                sp.dma_start(dst, src).then_inc(arrived, 16)

            def load_tables(g):
                if g >= 2:
                    sp.wait_ge(cosd, g - 1)
                    sp.wait_ge(sind, g - 1)
                for dst, src in ((cos_sb, cos), (sin_sb, sin)):
                    sp.dma_start(dst[:, g % 2], src.rearrange("(t p) c -> p t c", p=P)[
                        :, TG * g:TG * g + TG, :]).then_inc(trig_in[g], 16)

            load_tables(0)
            load_tables(1)
            sp.wait_ge(vnext_zero, 1)
            for g in range(G):
                sp.wait_ge(v_ready, TG * (g + 1))
                a = max(1, TG * g)
                sp.dma_start(vnext[P - 1:P, a - 1:TG * g + TG - 1, :],
                             v[0:1, a:TG * g + TG, :]).then_inc(vnext_in[g], 16)
                if g + 2 < G:
                    load_tables(g + 2)
            for j in range(J1, len(JOBS)):
                t0, nt = JOBS[j]
                sp.wait_ge(xf_ready, j + 1)
                sp.dma_start(o_t[:, t0:t0 + nt, :], xs[:, t0:t0 + nt, :]).then_inc(stored, 16)
            sp.wait_ge(stored, 16 * len(MLP_JOBS[1]))

        @block.gpsimd
        def _(pool):
            nc.gpsimd.memset(ones[:], 1.0).then_inc(warm, 1)
            nc.gpsimd.memset(mhalf[:], -0.5)
            nc.gpsimd.memset(above[:], -1.0)
            nc.gpsimd.memset(fives[:], STEPS / 2 / P).then_inc(consts, 1)
            for step in plan["pool"]:
                if step[0] == "rstd":
                    n, g = step[1:]
                    t0, nt = NORM_JOBS[n][g]
                    ts = slice(t0, t0 + nt)
                    pool.wait_ge(mom_ready[n], g + 1)
                    nc.gpsimd.tensor_scalar_add(veps[:, n, ts], mom[:, n, ts, 1], EPS_LN).then_inc(veps_ready[n], 1)

                    if engine_of["norm", n, g] == "act":
                        nc.gpsimd.tensor_scalar(nmean[:, n, ts], mom[:, n, ts, 0], -1.0, None, ALU.mult).then_inc(
                            nmean_ready[n], 1)
                    pool.wait_ge(veps_ready[n], g + 1)
                    pool.wait_ge(consts, 1)
                    nc.gpsimd.tensor_tensor(rstd[:, n, ts], veps[:, n, ts], mhalf[:, 0:nt],
                                            ALU.pow).then_inc(rstd_ready[n], 1)
                elif step[0] == "nmr":
                    n, g = step[1:]
                    t0, nt = NORM_JOBS[n][g]
                    ts = slice(t0, t0 + nt)
                    pool.wait_ge(nmean_ready[n], on_act_before(n, g) + 1)
                    pool.wait_ge(rstd_ready[n], g + 1)
                    nc.gpsimd.tensor_tensor(nmr[:, n, ts], nmean[:, n, ts], rstd[:, n, ts],
                                            ALU.mult).then_inc(nmr_ready[n], 1)
                elif step[0] == "bias":
                    g = step[1]
                    pool.wait_ge(*done["norm", 0, g])
                    if g == 0:
                        pool.wait_ge(small_in, 48)
                    xg = xs[:, TG * g:TG * g + TG, :]
                    nc.gpsimd.tensor_tensor(xg, xg, bias[:].unsqueeze(1).to_broadcast([P, TG, C]),
                                            ALU.add).then_inc(xb_ready, 1)
                elif step[0] == "w_lo":
                    k = step[1]
                    o, n = WEIGHTS[k]
                    pool.wait_ge(w_hi, k + 1)
                    nc.gpsimd.tensor_tensor(wl[:, o:o + n], RAW[k], wh[:, o:o + n],
                                            ALU.subtract).then_inc(w_lo[k], 1)
                elif step[0] == "vnext_zero":
                    nc.gpsimd.memset(vnext[:], 0.0).then_inc(vnext_zero, 1)
                elif step[0] == "half_id":
                    pool.wait_ge(id_in, 16)
                    nc.gpsimd.tensor_scalar(half_id[:], id_sb[:], 0.5, None, ALU.mult).then_inc(half_ready_id, 1)
                elif step[0] == "sq":
                    j, m = step[1:3]
                    width = P * JOBS[j][1]
                    pool.wait_ge(relu_ready, M * j + m + 1)
                    if j >= 2:
                        pool.wait_ge(y_ready, j - 1)
                    if j == 0:
                        raw_used(pool)
                    r = relu[:, m % 2, 0:width]
                    nc.gpsimd.tensor_tensor(hid[:, j % 2, m, 0:width], r, r, ALU.mult).then_inc(*one(done["sq", j, m]))
                elif step[0] == "lo":
                    lane, j = lane_job(*step[1:])
                    width = P * NORM_JOBS[step[1]][step[2]][1]
                    pool.wait_ge(xfull_ready[lane], full_number(step))
                    pool.wait_ge(hi_ready[lane], j + 1)
                    if j:
                        pool.wait_ge(lo_ready[lane], j)
                    nc.gpsimd.tensor_tensor(xl[lane][:, j % 2, 0:width], xfull[:, lane, 0:width],
                                            xh[lane][:, j % 2, 0:width], ALU.subtract).then_inc(lo_ready[lane], 1)
                elif step[0] == "qk_lo":
                    g, k = step[1:]
                    hi, lo = ((qh, ql), (kh, kl))[k]
                    pool.wait_ge(qkfull_ready, full_number(step))
                    pool.wait_ge(qkhi_ready, 2 * g + k + 1)
                    if g or k:
                        pool.wait_ge(qklo_ready, 2 * g + k)
                    nc.gpsimd.tensor_tensor(lo[:, W * g:W * g + W], qkfull[:, k, :], hi[:, W * g:W * g + W],
                                            ALU.subtract).then_inc(qklo_ready, 1)
                elif step[0] == "rot":
                    rotate(pool, *step[1:])
                elif step[0] == "sin":
                    g = step[1]
                    pool.wait_ge(v_ready, TG * (g + 1))
                    pool.wait_ge(trig_in[g], 32)
                    if g:
                        pool.wait_ge(half_ready[0], g)
                        pool.wait_ge(half_ready[1], g)
                    nc.gpsimd.tensor_tensor(
                        rsin[:].rearrange("p t (a c) -> p t a c", a=2),
                        qk[:, g % 2].rearrange("p t (a c) -> p t a c", a=2),
                        sin_sb[:, g % 2].unsqueeze(2).to_broadcast([P, TG, 2, C]), ALU.mult).then_inc(sind, 1)

        @block.scalar
        def _(act):
            act.dma_start(id_sb[:], ident).then_inc(id_in, 16)
            act.dma_start(RAW[0], w_qkv).then_inc(wa_in, 16)
            act.dma_start(heads_sb[:], heads).then_inc(small_in, 16)
            act.dma_start(wp[:], w_proj).then_inc(small_in, 16)
            act.dma_start(bias[:], b_proj.partition_broadcast(P)).then_inc(small_in, 16)
            for step in plan["act"]:
                if step[0] == "w_hi":
                    o, n = WEIGHTS[step[1]]
                    act.wait_ge((wa_in, wf_in, wr_in)[step[1]], 16)
                    nc.scalar.copy(wh[:, o:o + n], RAW[step[1]]).then_inc(w_hi, 1)
                elif step[0] == "norm":
                    n, g = step[1:3]
                    lane, j = lane_job(n, g)
                    t0, nt = NORM_JOBS[n][g]
                    act.wait_ge(nmr_ready[n], on_act_before(n, g) + 1)
                    if j >= 2:
                        act.wait_ge(xT_ready[lane], j - 1)
                    for t in range(nt):
                        last = nc.scalar.activation(
                            xn[lane][:, j % 2, t, :], xs[:, t0 + t, :], ACT.Identity,
                            bias=nmr[:, n, t0 + t:t0 + t + 1], scale=rstd[:, n, t0 + t:t0 + t + 1])
                    last.then_inc(*one(done["norm", n, g]))
                elif step[0] == "hi":
                    lane, j = lane_job(*step[1:])
                    bank = (MB, H1)[j % 2] if step[1] == 0 else MB
                    act.wait_ge(xT_ready[lane], j + 1)
                    lane_used(act, lane, j)
                    width = P * NORM_JOBS[step[1]][step[2]][1]
                    lone = step[1] % 2 == 1 and width == P
                    nc.scalar.copy(x_one[:, j % 2] if lone else xh[lane][:, j % 2, 0:width],
                                   bank[:, 0:width]).then_inc(hi_ready[lane], 1)
                elif step[0] == "full":
                    lane, j = lane_job(*step[1:])
                    bank = (MB, H1)[j % 2] if step[1] == 0 else MB
                    width = P * NORM_JOBS[step[1]][step[2]][1]
                    act.wait_ge(xT_ready[lane], j + 1)
                    if j:
                        act.wait_ge(lo_ready[lane], j)
                    nc.scalar.copy(xfull[:, lane, 0:width], bank[:, 0:width]).then_inc(xfull_ready[lane], 1)
                elif step[0] == "qk_full":
                    g, k = step[1:]
                    act.wait_ge(tqk_ready, 2 * g + k + 1)
                    act.wait_ge(aT_ready, G)
                    if g or k:
                        act.wait_ge(qklo_ready, 2 * g + k)
                    nc.scalar.copy(qkfull[:, k, :], (P0, P1)[k][:]).then_inc(qkfull_ready, 1)
                elif step[0] == "q_exp":
                    g = step[1]
                    act.wait_ge(q_ready, g + 1)
                    if g >= 2:
                        act.wait_ge(qphi_ready, g - 1)
                    nc.scalar.activation(ebuf[:, g % 2, :], O[:], ACT.Exp).then_inc(eq_ready, 1)
                    nc.scalar.activation(rbuf[:, g % 2, :], O[:], ACT.Relu).then_inc(rq_ready, 1)
                elif step[0] == "kv_exp":
                    g, pr = step[1:]
                    n = 2 * g + pr
                    bank = ((S0, S1), (P0, P1))[g % 2][pr][:].rearrange("p (t c) -> p t c", t=2)
                    act.wait_ge(kv_ready, n + 1)
                    if n >= 2:
                        act.wait_ge(kphi_ready, n - 1)
                    nc.scalar.activation(ek[:, pr], bank[:, :, 0:C], ACT.Exp).then_inc(ek_ready, 1)
                    nc.scalar.activation(rk[:, pr], bank[:, :, 0:C], ACT.Relu).then_inc(rk_ready, 1)
                    nc.scalar.copy(vone[:, 2 * n:2 * n + 2, 0:C], bank[:, :, C:2 * C]).then_inc(vone_ready, 1)
                elif step[0] == "aT_copy":
                    g = step[1]
                    act.wait_ge(aT_ready, g + 1)
                    if g >= 2:
                        act.wait_ge(pr_ready, g - 1)
                    nc.scalar.copy(rbuf[:, g % 2, :], O[:]).then_inc(aTs_ready, 1)
                elif step[0] == "relu":
                    j, m = step[1:]
                    n = M * j + m
                    width = P * JOBS[j][1]
                    act.wait_ge(h_ready, n + 1)
                    if n >= 2:
                        act.wait_ge(*done["sq", *divmod(n - 2, M)])
                    nc.scalar.activation(relu[:, m % 2, 0:width], (H0, H1)[m % 2][:, 0:width],
                                         ACT.Relu).then_inc(relu_ready, 1)
                elif step[0] == "sq":
                    j, m = step[1:]
                    width = P * JOBS[j][1]
                    act.wait_ge(relu_ready, M * j + m + 1)
                    act.wait_ge(relu_ready, M * j + m + 1)
                    if j >= 2:
                        act.wait_ge(y_ready, j - 1)
                    if j == 0:
                        raw_used(act)
                    nc.scalar.activation(hid[:, j % 2, m, 0:width], relu[:, m % 2, 0:width],
                                         ACT.Square).then_inc(*one(done["sq", j, m]))
                elif step[0] == "y" or step[0] == "u_first":
                    j = step[1]
                    width = P * JOBS[j][1]
                    act.wait_ge(y_ready, j + 1)
                    if j >= 2:
                        act.wait_ge(xf_ready, j - 1)
                    if step[0] == "y":
                        nc.scalar.copy(y[:, j % 2, 0:width], MB[:, 0:width]).then_inc(ysb_ready, 1)
                    else:
                        nc.scalar.activation(u_first[:, j % 2, 0:width], MB[:, 0:width], ACT.Copy,
                                             scale=1.0 + BETA).then_inc(u_first_ready, 1)
                elif step[0] == "sign":
                    j, k = step[1:]
                    width = P * JOBS[j][1]
                    if k == 0:
                        if j == 0:
                            act.wait_ge(consts, 1)
                        elif sign_user(j) is not None:
                            act.wait_ge(count_ready, sign_user(j) + 1)
                        act.wait_ge(ysb_ready, j + 1)
                        src = y[:, j % 2, 0:width]
                    else:
                        act.wait_ge(mem_ready, MEMS * j + 2 * k - 1)
                        src = mem[:, (k - 1) % 2, 0:width]
                    nc.scalar.activation(sign[:, k, sign_columns(j)], src, ACT.Sign, bias=above[:, 0:1],
                                         scale=JUST_BELOW_1 if k == 0 else -JUST_BELOW_1).then_inc(sign_ready, 1)
                elif step[0] == "qkv_copy":
                    g, t = step[1:]
                    if g >= 2 and t == 0:
                        act.wait_ge(cosd, g - 1)
                        act.wait_ge(sind, g - 1)
                    n = TG * g + t
                    bank = (S0, S1)[n % 2]
                    act.wait_ge(qkv_ready, n + 1)
                    nc.scalar.copy(qk[:, g % 2, t, :], bank[:, 0:2 * C])
                    nc.scalar.copy(v[:, n, :], bank[:, 2 * C:3 * C]).then_inc(v_ready, 1)
                elif step[0] == "qk_hi":
                    g, k = step[1:]
                    dst, bank = ((qh, P0), (kh, P1))[k]
                    act.wait_ge(tqk_ready, 2 * g + k + 1)
                    nc.scalar.copy(dst[:, W * g:W * g + W], bank[:]).then_inc(qkhi_ready, 1)
                elif step[0] == "e":
                    i, p = step[1:]
                    a, b = exp_pieces(i)[p]
                    s = scores[i % 2]
                    act.wait_ge(m_ready, i + 1)
                    nc.scalar.activation(s[:, a:b], s[:, a:b], ACT.Exp, bias=negm[:, i:i + 1], scale=1.0,
                                         accum_out=psums[:, i, p:p + 1]).then_inc(e_ready, 1)
                elif step[0] == "pt_copy":
                    i, jg = step[1:3]
                    n = turn_no[i, jg]
                    nb = min(TG, i + 1 - TG * jg)
                    act.wait_ge(pt_ready, n + 1)
                    if n >= 3:
                        act.wait_ge(pv_ready, n - 2)
                    nc.scalar.copy(pt[:, n % 3, 0:P * nb], (P0, P1)[n % 2][:, 0:P * nb]).then_inc(*one(done["pt_copy", i, jg]))

        @block.vector
        def _(dve):
            nc.vector.memset(vone[:, :, C:C + 1], 1.0).then_inc(vone_set, 1)
            for step in plan["dve"]:
                if step[0] == "stats":
                    n, g = step[1:]
                    t0, nt = NORM_JOBS[n][g]
                    if n == 0:
                        dve.wait_ge(x_in[g], 16)
                    elif n == 1:
                        dve.wait_ge(x1_ready, (t0 + nt - 1) // TG + 1)
                    elif n == 2:
                        dve.wait_ge(xf_ready, next(k for k, (a, b) in enumerate(JOBS) if a + b >= t0 + nt) + 1)
                    else:
                        dve.wait_ge(x3_ready, t0 + nt)
                    for t in range(t0, t0 + nt):
                        last = nc.vector.bn_stats(stat[:, n, t, :], xs[:, t, :])
                    last.then_inc(bn_done[n], 1)
                    dve.wait_ge(bn_done[n], g + 1)
                    for t in range(t0, t0 + nt):
                        last = nc.vector.bn_aggr(mom[:, n, t, :], stat[:, n, t, :])
                    last.then_inc(mom_ready[n], 1)
                elif step[0] == "w_lo":
                    k = step[1]
                    o, n = WEIGHTS[k]
                    dve.wait_ge(w_hi, k + 1)
                    nc.vector.tensor_tensor(wl[:, o:o + n], RAW[k], wh[:, o:o + n],
                                            ALU.subtract).then_inc(w_lo[k], 1)
                elif step[0] == "norm":
                    n, g = step[1:3]
                    lane, j = lane_job(n, g)
                    t0, nt = NORM_JOBS[n][g]
                    dve.wait_ge(rstd_ready[n], g + 1)
                    if j >= 2:
                        dve.wait_ge(xT_ready[lane], j - 1)
                    for t in range(nt):
                        k = t0 + t
                        last = nc.vector.tensor_scalar(xn[lane][:, j % 2, t, :], xs[:, k, :], mom[:, n, k, 0:1],
                                                       rstd[:, n, k:k + 1], ALU.subtract, ALU.mult)
                    last.then_inc(*one(done["norm", n, g]))
                elif step[0] == "lo":
                    lane, j = lane_job(*step[1:])
                    bank = (MB, H1)[j % 2] if step[1] == 0 else MB
                    dve.wait_ge(hi_ready[lane], j + 1)
                    if j:
                        dve.wait_ge(lo_ready[lane], j)
                    width = P * NORM_JOBS[step[1]][step[2]][1]
                    nc.vector.tensor_tensor(xl[lane][:, j % 2, 0:width], bank[:, 0:width], xh[lane][:, j % 2, 0:width],
                                            ALU.subtract).then_inc(lo_ready[lane], 1)
                elif step[0] == "q_phi":
                    g = step[1]
                    dve.wait_ge(rq_ready, g + 1)
                    nc.vector.scalar_tensor_tensor(
                        out=qphi[:, W * g:W * g + W], in0=ebuf[:, g % 2, :], scalar=1.0, in1=rbuf[:, g % 2, :],
                        op0=ALU.min, op1=ALU.add).then_inc(qphi_ready, 1)
                elif step[0] == "k_phi":
                    g, pr = step[1:]
                    n = 2 * g + pr
                    dve.wait_ge(rk_ready, n + 1)
                    nc.vector.scalar_tensor_tensor(
                        out=kphi[:, 2 * C * n:2 * C * n + 2 * C].rearrange("p (t c) -> p t c", t=2),
                        in0=ek[:, pr], scalar=1.0, in1=rk[:, pr], op0=ALU.min, op1=ALU.add).then_inc(kphi_ready, 1)
                elif step[0] == "diag":
                    dve.wait_ge(small_in, 48)
                    dve.wait_ge(sum_ready, 1)
                    nc.vector.tensor_tensor(bdkv[:], H0[:, 0:C], heads_sb[:, 0:C], ALU.mult).then_inc(diag_ready, 1)
                    nc.vector.tensor_scalar(bdks[:], heads_sb[:, C:C + HEADS], H0[:, C:C + 1], None,
                                            ALU.mult).then_inc(diag_ready, 1)
                elif step[0] == "heads":
                    g = step[1]
                    dve.wait_ge(ao_ready, g + 1)
                    top, bottom = ((P0, P1), (S0, S1))[g % 2]
                    nc.vector.tensor_scalar(den[:], bottom[:, 0:TG * HEADS], EPS_ATT, None, ALU.add).then_inc(den_ready, 1)
                    dve.wait_ge(den_ready, g + 1)
                    nc.vector.reciprocal(rec[:], den[:]).then_inc(rec_ready, 1)
                    dve.wait_ge(rec_ready, g + 1)
                    if g >= 2:
                        dve.wait_ge(aT_ready, g - 1)
                    else:
                        dve.wait_ge(qphi_ready, G)
                    nc.vector.tensor_tensor(
                        ebuf[:, g % 2, :].rearrange("p (h d) -> p h d", d=HD),
                        top[:].rearrange("p (h d) -> p h d", d=HD),
                        rec[:].unsqueeze(2).to_broadcast([P, TG * HEADS, HD]), ALU.mult).then_inc(heads_ready, 1)
                elif step[0] == "x1":
                    g = step[1]
                    dve.wait_ge(pr_ready, g + 1)
                    dve.wait_ge(xb_ready, g + 1)
                    xg = xs[:, TG * g:TG * g + TG, :].rearrange("p t c -> p (t c)")
                    nc.vector.tensor_tensor(xg, (P1, S1)[g % 2][:], xg, ALU.add).then_inc(x1_ready, 1)
                elif step[0] == "mem":
                    j, k = step[1:]
                    width = P * JOBS[j][1]
                    ys = y[:, j % 2, 0:width]
                    n = MEMS * j + max(0, 2 * k - 1)
                    if k == 0:
                        dve.wait_ge(u_first_ready, j + 1)
                        if j:
                            dve.wait_ge(mem_ready, n)
                        old, sgn, new = ys, 1.0, u_first[:, j % 2, 0:width]
                    else:
                        old, sgn, new = mem[:, (k - 1) % 2, 0:width], -1.0, u[:, 0:width]
                        dve.wait_ge(mem_ready, n)
                        nc.vector.scalar_tensor_tensor(out=new, in0=old, scalar=sgn * BETA, in1=ys,
                                                       op0=ALU.mult, op1=ALU.add).then_inc(mem_ready, 1)
                        dve.wait_ge(mem_ready, n + 1)
                    if k >= 2:
                        dve.wait_ge(sign_ready, STEPS * j + k)
                    elif j:
                        dve.wait_ge(sign_ready, STEPS * (j - 1) + k + 4)
                    nc.vector.scalar_tensor_tensor(
                        out=mem[:, k % 2, 0:width], in0=old, scalar=sgn * THRESHOLD, in1=new,
                        op0=ALU.is_gt if k == 0 else ALU.is_lt, op1=ALU.subtract).then_inc(mem_ready, 1)
                elif step[0] == "xf":
                    j = step[1]
                    t0, nt = JOBS[j]
                    dve.wait_ge(count_ready, j + 1)
                    xg = xs[:, t0:t0 + nt, :].rearrange("p t c -> p (t c)")
                    nc.vector.scalar_tensor_tensor(out=xg, in0=H0[:, 0:P * nt], scalar=1.0 / STEPS, in1=xg,
                                                   op0=ALU.mult, op1=ALU.add).then_inc(xf_ready, 1)
                elif step[0] == "cos":
                    g = step[1]
                    dve.wait_ge(v_ready, TG * (g + 1))
                    dve.wait_ge(trig_in[g], 32)
                    if g >= 2:
                        dve.wait_ge(tqk_ready, 2 * (g - 1))
                    r = rot[:, g % 2].rearrange("p t (a c) -> p t a c", a=2)
                    nc.vector.tensor_tensor(
                        r, qk[:, g % 2].rearrange("p t (a c) -> p t a c", a=2),
                        cos_sb[:, g % 2].unsqueeze(2).to_broadcast([P, TG, 2, C]), ALU.mult).then_inc(cosd, 1)
                elif step[0] == "rot":
                    rotate(dve, *step[1:])
                elif step[0] == "sq":
                    j, m = step[1:3]
                    width = P * JOBS[j][1]
                    dve.wait_ge(relu_ready, M * j + m + 1)
                    if j >= 2:
                        dve.wait_ge(y_ready, j - 1)
                    if j == 0:
                        raw_used(dve)
                    r = relu[:, m % 2, 0:width]
                    nc.vector.tensor_tensor(hid[:, j % 2, m, 0:width], r, r, ALU.mult).then_inc(*one(done["sq", j, m]))
                elif step[0] == "qk_lo":
                    g, k = step[1:]
                    hi, lo, bank = ((qh, ql, P0), (kh, kl, P1))[k]
                    dve.wait_ge(qkhi_ready, 2 * g + k + 1)
                    if g or k:
                        dve.wait_ge(qklo_ready, 2 * g + k)
                    nc.vector.tensor_tensor(lo[:, W * g:W * g + W], bank[:], hi[:, W * g:W * g + W],
                                            ALU.subtract).then_inc(qklo_ready, 1)
                elif step[0] == "pt_copy":
                    i, jg = step[1:3]
                    n = turn_no[i, jg]
                    nb = min(TG, i + 1 - TG * jg)
                    dve.wait_ge(pt_ready, n + 1)
                    if n >= 3:
                        dve.wait_ge(pv_ready, n - 2)
                    nc.vector.tensor_copy(pt[:, n % 3, 0:P * nb], (P0, P1)[n % 2][:, 0:P * nb]).then_inc(
                        *one(done["pt_copy", i, jg]))
                elif step[0] == "score_copy":
                    i, c = step[1:]
                    cuts = score_chunks(i)
                    if i >= 2 and c == 0:
                        dve.wait_ge(pt_ready, turn_no[i - 2, (i - 2) // TG] + 1)
                        dve.wait_ge(osb_ready, i - 1)
                    elif i < 2 and c == 0:
                        dve.wait_ge(mask_in, 16)
                        dve.wait_ge(ao_ready, G)
                    a, b = cuts[c]
                    n = chunk_no[i, c]
                    dve.wait_ge(s_ready, n + 1)
                    bank = (S0, S1)[n % 2][:, 0:b - a]
                    if c < len(cuts) - 1:
                        nc.vector.tensor_scalar(scores[i % 2][:, a:b], bank, SCALE, MASKED, ALU.mult, ALU.max,
                                                accum_out=cmax[:, i, c:c + 1]).then_inc(sc_ready, 1)
                        continue
                    m0 = MASK_LEAD - (P * i - a)
                    nc.vector.tensor_tensor_reduce(scores[i % 2][:, a:b], bank, mask_sb[:, m0:m0 + b - a], SCALE,
                                                   MASKED, ALU.add, ALU.max, cmax[:, i, c:c + 1]).then_inc(sc_ready, 1)
                    dve.wait_ge(sc_ready, n + 1)
                    nc.vector.tensor_reduce(negm[:, i:i + 1], cmax[:, i, 0:len(cuts)], AX_X, ALU.max,
                                            negate=True).then_inc(m_ready, 1)
                elif step[0] == "row_sum":
                    i = step[1]
                    np_ = len(exp_pieces(i))
                    dve.wait_ge(e_ready, piece_no[i, np_ - 1] + 1)
                    total = psums[:, i, 0:1]
                    if np_ > 1:
                        total = psum_all[:, i:i + 1]
                        nc.vector.tensor_reduce(total, psums[:, i, 0:np_], AX_X, ALU.add).then_inc(ps_ready, 1)
                        dve.wait_ge(ps_ready, sum(len(exp_pieces(k)) > 1 for k in range(i + 1)))
                    nc.vector.reciprocal(rsum[:, i:i + 1], total).then_inc(rs_ready, 1)
                elif step[0] == "o":
                    i = step[1]
                    dve.wait_ge(pv_ready, turn_no[i, i // TG] + 1)
                    o = O[:, C * (i % TG):C * (i % TG) + C]
                    if i < T - 1:
                        dve.wait_ge(vnext_in[(i + 1) // TG], 16)
                        if i >= 2:
                            dve.wait_ge(x3_ready, i - 1)
                        nc.vector.scalar_tensor_tensor(
                            out=osb[:, i % 2, :], in0=vnext[:, i, :], scalar=scores[i % 2][:, P * (i + 1):P * (i + 1) + 1],
                            in1=o, op0=ALU.mult, op1=ALU.add).then_inc(osb_ready, 1)
                        dve.wait_ge(osb_ready, i + 1)
                        o = osb[:, i % 2, :]
                    dve.wait_ge(rs_ready, i + 1)
                    nc.vector.scalar_tensor_tensor(out=xs[:, i, :], in0=o, scalar=rsum[:, i:i + 1], in1=xs[:, i, :],
                                                   op0=ALU.mult, op1=ALU.add).then_inc(x3_ready, 1)

        @block.tensor
        def _(pe):
            reader = {}

            def claim(bank):
                if bank.name in reader:
                    pe.wait_ge(*reader[bank.name])

            def split_product(dst, stationary, moving):
                (sh, sl), (mh, ml) = stationary, moving
                nc.tensor.matmul(dst, sh, mh, start=True, stop=False)
                nc.tensor.matmul(dst, sh, ml, start=False, stop=False)
                return nc.tensor.matmul(dst, sl, mh, start=False, stop=True)

            pe.wait_ge(warm, 1)
            for _ in range(WARM_UP):
                nc.tensor.matmul(H0[:], ones[:, 0:P], ones[:], start=True, stop=True)
            pe.wait_ge(id_in, 16)
            for step in plan["pe"]:
                if step[0] == "turn":
                    n, g = step[1:]
                    lane, j = lane_job(n, g)
                    bank = (MB, H1)[j % 2] if n == 0 else MB
                    pe.wait_ge(*done["norm", n, g])
                    claim(bank)
                    for t in range(NORM_JOBS[n][g][1]):
                        last = nc.tensor.transpose(bank[:, C * t:C * t + C], xn[lane][:, j % 2, t, :], id_sb[:])
                    last.then_inc(xT_ready[lane], 1)
                    lone = n % 2 == 1 and NORM_JOBS[n][g][1] == 1
                    if lone:
                        reader[bank.name] = (hi_ready[lane], j + 1)
                    else:
                        reader[bank.name] = bank_freed(("lo", n, g), (lo_ready[lane], j + 1), xfull_ready[lane])
                elif step[0] == "q":
                    g = step[1]
                    pe.wait_ge(lo_ready[0], g + 1)
                    pe.wait_ge(w_lo[0], 1)
                    claim(O)
                    split_product(O[:], (wh[:, 0:C], wl[:, 0:C]),
                                  (xh[0][:, g % 2, :], xl[0][:, g % 2, :])).then_inc(q_ready, 1)
                    reader[O.name] = (rq_ready, g + 1)
                elif step[0] == "kv":
                    g, pr = step[1:]
                    pe.wait_ge(lo_ready[0], g + 1)
                    pe.wait_ge(w_lo[0], 1)
                    bank = ((S0, S1), (P0, P1))[g % 2][pr]
                    claim(bank)
                    for t in range(2):
                        o = C * (2 * pr + t)
                        last = split_product(
                            bank[:, 2 * C * t:2 * C * t + 2 * C],
                            (xh[0][:, g % 2, o:o + C], xl[0][:, g % 2, o:o + C]), (wh[:, C:3 * C], wl[:, C:3 * C]))
                    last.then_inc(kv_ready, 1)
                    reader[bank.name] = (vone_ready, 2 * g + pr + 1)
                elif step[0] == "acc":
                    g = step[1]
                    if g == 0:
                        pe.wait_ge(vone_set, 1)
                    pe.wait_ge(kphi_ready, 2 * g + 2)
                    pe.wait_ge(vone_ready, 2 * g + 2)
                    for t in range(TG * g, TG * g + TG):
                        last = nc.tensor.matmul(H0[:, 0:C + 1], kphi[:, C * t:C * t + C], vone[:, t, :],
                                                start=(t == 0), stop=(t == T - 1))
                    if g == G - 1:
                        last.then_inc(sum_ready, 1)
                        reader[H0.name] = (diag_ready, 2)
                elif step[0] == "ao":
                    g = step[1]
                    pe.wait_ge(diag_ready, 2)
                    pe.wait_ge(qphi_ready, g + 1)
                    top, bottom = ((P0, P1), (S0, S1))[g % 2]
                    claim(top)
                    claim(bottom)
                    for t in range(TG):
                        q_t = qphi[:, W * g + P * t:W * g + P * t + P]
                        nc.tensor.matmul(top[:, C * t:C * t + C], q_t, bdkv[:], start=True, stop=True)
                        last = nc.tensor.matmul(bottom[:, HEADS * t:HEADS * t + HEADS], q_t, bdks[:], start=True, stop=True)
                    last.then_inc(ao_ready, 1)
                    reader[top.name] = reader[bottom.name] = (heads_ready, g + 1)
                elif step[0] == "at":
                    g = step[1]
                    pe.wait_ge(heads_ready, g + 1)
                    claim(O)
                    for t in range(TG):
                        last = nc.tensor.transpose(O[:, C * t:C * t + C], ebuf[:, g % 2, C * t:C * t + C], id_sb[:])
                    last.then_inc(aT_ready, 1)
                    reader[O.name] = (aTs_ready, g + 1)
                elif step[0] == "pr":
                    g = step[1]
                    pe.wait_ge(aTs_ready, g + 1)
                    bank = (P1, S1)[g % 2]
                    claim(bank)
                    for t in range(TG):
                        last = nc.tensor.matmul(bank[:, C * t:C * t + C], rbuf[:, g % 2, C * t:C * t + C], wp[:],
                                                start=True, stop=True)
                    last.then_inc(pr_ready, 1)
                    reader[bank.name] = (x1_ready, g + 1)
                elif step[0] == "f1":
                    j, m = step[1:]
                    bank = (H0, H1)[m % 2]
                    o = f_of + P * m
                    claim(bank)
                    width = P * JOBS[j][1]
                    if width == P:
                        pe.wait_ge(hi_ready[1], j + 1)
                        last = nc.tensor.matmul(bank[:, 0:P], w_fc_sb[:, P * m:P * m + P], x_one[:, j % 2], start=True,
                                                stop=True)
                        last.then_inc(h_ready, 1)
                        reader[bank.name] = (relu_ready, M * j + m + 1)
                        continue
                    pe.wait_ge(w_lo[1], 1)
                    pe.wait_ge(lo_ready[1], j + 1)
                    split_product(bank[:, 0:width], (wh[:, o:o + P], wl[:, o:o + P]),
                                  (xh[1][:, j % 2, 0:width], xl[1][:, j % 2, 0:width])).then_inc(h_ready, 1)
                    reader[bank.name] = (relu_ready, M * j + m + 1)
                elif step[0] == "f2":
                    j, t = step[1:]
                    if t == 0:
                        if j == 0:
                            pe.wait_ge(wd_in, 16)
                        for m in range(M):
                            pe.wait_ge(*done["sq", j, m])
                        claim(MB)
                    for m in range(M):
                        last = nc.tensor.matmul(MB[:, C * t:C * t + C], hid[:, j % 2, m, P * t:P * t + P],
                                                wd[:, m, :], start=(m == 0), stop=(m == M - 1))
                    if t == JOBS[j][1] - 1:
                        last.then_inc(y_ready, 1)
                        reader[MB.name] = (u_first_ready, j + 1)
                elif step[0] == "count":
                    j = step[1]
                    width = P * JOBS[j][1]
                    pe.wait_ge(consts, 1)
                    pe.wait_ge(half_ready_id, 1)
                    claim(H0)
                    nc.tensor.matmul(H0[:, 0:width], fives[:], ones[:, 0:width], start=True, stop=False)
                    for k in range(STEPS):
                        pe.wait_ge(sign_ready, STEPS * j + k + 1)
                        last = nc.tensor.matmul(H0[:, 0:width], half_id[:], sign[:, k, sign_columns(j)], start=False, stop=(k == STEPS - 1))
                    last.then_inc(count_ready, 1)
                    reader[H0.name] = (xf_ready, j + 1)
                elif step[0] == "qkv":
                    g, t = step[1:]
                    n = TG * g + t
                    bank = (S0, S1)[n % 2]
                    pe.wait_ge(w_lo[2], 1)
                    pe.wait_ge(lo_ready[0], G + g + 1)
                    claim(bank)
                    split_product(bank[:, 0:3 * C], (xh[0][:, g % 2, P * t:P * t + P], xl[0][:, g % 2, P * t:P * t + P]),
                                  (wh[:, r_of:r_of + WR], wl[:, r_of:r_of + WR])).then_inc(qkv_ready, 1)
                    reader[bank.name] = (v_ready, n + 1)
                elif step[0] == "tqk":
                    g, k = step[1:]
                    bank = (P0, P1)[k]
                    pe.wait_ge(half_ready[0], g + 1)
                    pe.wait_ge(half_ready[1], g + 1)
                    claim(bank)
                    for t in range(TG):
                        last = nc.tensor.transpose(bank[:, P * t:P * t + P], rot[:, g % 2, t, C * k:C * k + C], id_sb[:])
                    last.then_inc(tqk_ready, 1)
                    reader[bank.name] = bank_freed(("qk_lo", g, k), (qklo_ready, 2 * g + k + 1), qkfull_ready)
                elif step[0] == "s":
                    i, c = step[1:]
                    a, b = score_chunks(i)[c]
                    n = chunk_no[i, c]
                    bank = (S0, S1)[n % 2]
                    if c == 0:
                        pe.wait_ge(qklo_ready, 2 * (min(i + 1, T - 1) // TG) + 2)
                    claim(bank)
                    split_product(bank[:, 0:b - a], (qh[:, P * i:P * i + P], ql[:, P * i:P * i + P]),
                                  (kh[:, a:b], kl[:, a:b])).then_inc(s_ready, 1)
                    reader[bank.name] = (sc_ready, n + 1)
                elif step[0] == "pt":
                    i, jg = step[1:]
                    n = turn_no[i, jg]
                    nb = min(TG, i + 1 - TG * jg)
                    end = P * (TG * jg + nb)
                    piece = next(p for p, (a, b) in enumerate(exp_pieces(i)) if end <= b)
                    bank = (P0, P1)[n % 2]
                    pe.wait_ge(e_ready, piece_no[i, piece] + 1)
                    claim(bank)
                    for b in range(nb):
                        k0 = P * (TG * jg + b)
                        last = nc.tensor.transpose(bank[:, P * b:P * b + P], scores[i % 2][:, k0:k0 + P], id_sb[:])
                    last.then_inc(pt_ready, 1)
                    reader[bank.name] = done["pt_copy", i, jg]
                elif step[0] == "pv":
                    i, jg = step[1:]
                    n = turn_no[i, jg]
                    nb = min(TG, i + 1 - TG * jg)
                    pe.wait_ge(*done["pt_copy", i, jg])
                    if jg == 0:
                        claim(O)
                    for b in range(nb):
                        k = TG * jg + b
                        last = nc.tensor.matmul(O[:, C * (i % TG):C * (i % TG) + C], pt[:, n % 3, P * b:P * b + P],
                                                v[:, k, :], start=(k == 0), stop=(k == i))
                    last.then_inc(pv_ready, 1)
                    if k == i:
                        reader[O.name] = (x3_ready, i + 1)


def rotary_tables():
    i = np.arange(HALF, dtype=np.float32)
    theta = np.power(np.float32(10000.0), np.float32(-2.0) * i / np.float32(C)).astype(np.float32)
    ang = np.arange(N_TOK, dtype=np.float32)[:, None] * theta[None, :]
    c, s = np.cos(ang), np.sin(ang)
    return np.concatenate([c, c], 1), np.concatenate([s, -s], 1)


def score_mask():
    q, k = np.arange(P)[:, None], np.arange(MASK_W)[None, :] - MASK_LEAD
    return np.where(k <= q + EXTRA, 0.0, MASKED).astype(np.float32)


def head_masks():
    own = (np.arange(C)[:, None] // HD == np.arange(C)[None, :] // HD)
    per = (np.arange(C)[:, None] // HD == np.arange(HEADS)[None, :])
    return np.concatenate([own, per], 1).astype(np.float32)


def kernel(L0_attn_a_x, L0_attn_a_Wqkv, L0_attn_a_Wproj, L0_attn_a_bproj, L0_attn_b_Wq, L0_attn_b_Wk,
           L0_attn_b_Wv, L0_ffn_W_fc, L0_ffn_W_proj):
    import concourse.bacc as _bacc
    from concourse.bass_utils import run_bass_kernel_spmd as _run

    lay = np.ascontiguousarray
    order = np.concatenate([np.arange(0, C, 2), np.arange(1, C, 2)])
    rope_rows = np.concatenate([np.asarray(L0_attn_b_Wq)[order], np.asarray(L0_attn_b_Wk)[order],
                                np.asarray(L0_attn_b_Wv)])
    cos, sin = rotary_tables()
    arrays = {
        "x": lay(np.asarray(L0_attn_a_x).reshape(N_TOK, C)),
        "w_qkv": lay(np.asarray(L0_attn_a_Wqkv).T),
        "w_proj": lay(np.asarray(L0_attn_a_Wproj).T),
        "b_proj": lay(np.asarray(L0_attn_a_bproj)),
        "w_fc": lay(np.asarray(L0_ffn_W_fc).T),
        "w_down": lay(np.asarray(L0_ffn_W_proj).T.reshape(M, P, C).transpose(1, 0, 2).reshape(P, M * C)),
        "w_rope": lay(rope_rows.T),
        "cos": lay(cos.astype(np.float32)),
        "sin": lay(sin.astype(np.float32)),
        "ident": np.eye(P, dtype=np.float32),
        "mask": score_mask(),
        "heads": head_masks(),
    }
    nc = _bacc.Bacc("TRN2", target_bir_lowering=False, num_devices=1)
    args = [nc.dram_tensor(f"in_{n}", a.shape, mybir.dt.from_np(a.dtype), kind="ExternalInput").ap()
            for n, a in arrays.items()]
    args.append(nc.dram_tensor("out_x", (N_TOK, C), F32, kind="ExternalOutput").ap())
    hybrid_block(nc, *args)
    r = _run(nc, [{f"in_{n}": a for n, a in arrays.items()}], core_ids=[0])
    return r.results[0]["out_x"].reshape(1, N_TOK, C)
```
